# Optimizing a Trainium2 kernel written in Bass

```python
import numpy as np
import jax
import jax.numpy as jnp

def _softmax(x, axis=-1):
    return jax.nn.softmax(x, axis=axis)

def _gelu(x):
    return jax.nn.gelu(x, approximate=True)

def _silu(x):
    return jax.nn.silu(x)

def _sigmoid(x):
    return jax.nn.sigmoid(x)

def _layernorm(x, axis=-1, eps=1e-05):
    m = jnp.mean(x, axis=axis, keepdims=True)
    v = jnp.var(x, axis=axis, keepdims=True)
    return (x - m) / jnp.sqrt(v + eps)

def _scatter_add(tgt, idx, src, axis=0):
    return tgt.at[idx].add(src)

def _segment_sum(src, seg, n):
    return jax.ops.segment_sum(src, seg, n)
kernel_name = 'mk_adj_resnorm_d2_adj_r2_5ca61c'

def setup_inputs(seed: int=0):
    np.random.seed(seed)
    _w = jnp.asarray

    def _rec_inputs():
        import jax
        import jax.numpy as jnp
        _gk = jax.random.key(seed)
        x = -0.0005207 + 1.001 * jax.random.normal(jax.random.fold_in(_gk, 1), (8192, 128), jnp.float32)
        _w = (1.0 + jnp.arange(8192, dtype=jnp.float32)) ** (-0.5)
        _w = _w / _w.mean()
        _pij = jnp.clip(0.00195312 * _w[:, None] * _w[None, :], 0.0, 1.0)
        _a = jax.random.uniform(jax.random.fold_in(_gk, 2), (8192, 8192)) < _pij
        _a = jnp.logical_or(_a, jnp.eye(8192, dtype=bool))
        _af = _a.astype(jnp.float32)
        _af = _af * jax.random.uniform(jax.random.fold_in(_gk, 3), (8192, 8192), jnp.float32, 0.05, 1)
        adj = _af
        return (x, adj)
    x, adj = _rec_inputs()

    def _L0_gnn_setup():
        import jax, jax.numpy as jnp
        import numpy as np
        ALPHA = 0.1
        N, F = (8192, 128)
        key = jax.random.key(seed)
        k1, k2, k3 = jax.random.split(key, 3)
        x = jax.random.normal(k1, (N, F), dtype=jnp.float32)
        adj = jax.random.uniform(k2, (N, N), dtype=jnp.float32)
        h = jax.random.normal(k3, (N, F), dtype=jnp.float32)
        return {'x': x, 'adj': adj, 'h': h}
    _L0_gnn_all = _L0_gnn_setup()
    _L0_gnn_in = {k: v for k, v in _L0_gnn_all.items() if k in ('h',)}
    del _L0_gnn_all

    def _L1_gnn_setup():
        import jax, jax.numpy as jnp
        import numpy as np
        N, DIN, DOUT = (4096, 128, 128)
        NEG = -9000000000000000.0
        ALPHA = 0.2
        key = jax.random.key(seed)
        kx, ka, kw, ks, kr = jax.random.split(key, 5)
        X = jax.random.normal(kx, (N, DIN), dtype=jnp.float32)
        A = (jax.random.uniform(ka, (N, N)) < 0.01).astype(jnp.float32)
        A = A.at[jnp.arange(N), jnp.arange(N)].set(1.0)
        lim_w = float(np.sqrt(6.0 / (DIN + DOUT)))
        W = jax.random.uniform(kw, (DOUT, DIN), jnp.float32, -lim_w, lim_w)
        b = jnp.zeros((DOUT,), jnp.float32)
        lim_a = float(np.sqrt(6.0 / (DOUT + 1)))
        a_s = jax.random.uniform(ks, (DOUT, 1), jnp.float32, -lim_a, lim_a)
        a_r = jax.random.uniform(kr, (DOUT, 1), jnp.float32, -lim_a, lim_a)
        return {'X': X, 'A': A, 'W': W, 'b': b, 'a_s': a_s, 'a_r': a_r}
    _L1_gnn_all = _L1_gnn_setup()
    _L1_gnn_in = {k: v for k, v in _L1_gnn_all.items() if k in ('W', 'b', 'a_s', 'a_r')}
    del _L1_gnn_all
    return {'x': x, 'adj': adj, 'L0_gnn_h': _L0_gnn_in['h'], 'L1_gnn_W': _L1_gnn_in['W'], 'L1_gnn_b': _L1_gnn_in['b'], 'L1_gnn_a_s': _L1_gnn_in['a_s'], 'L1_gnn_a_r': _L1_gnn_in['a_r']}

def reference(x, adj, L0_gnn_h, L1_gnn_W, L1_gnn_b, L1_gnn_a_s, L1_gnn_a_r):
    import jax
    import jax.numpy as jnp

    def _L0_gnn_ref(x, adj, h):
        import jax, jax.numpy as jnp
        import numpy as np
        ALPHA = 0.1
        N, F = (8192, 128)
        return (1.0 - ALPHA) * (adj @ x) + ALPHA * h

    def _L1_gnn_ref(X, A, W, b, a_s, a_r):
        import jax, jax.numpy as jnp
        import numpy as np
        N, DIN, DOUT = (4096, 128, 128)
        NEG = -9000000000000000.0
        ALPHA = 0.2
        H = X @ W.T + b
        s = H @ a_s
        r = H @ a_r
        e = jax.nn.leaky_relu(A * s + A * r.T, negative_slope=ALPHA)
        masked = jnp.where(A > 0, e, NEG)
        att = jax.nn.softmax(masked, axis=1)
        H_out = att @ H
        return H_out
    x = _layernorm(x + _L0_gnn_ref(x, adj, L0_gnn_h), axis=-1)
    x = _layernorm(x + _L1_gnn_ref(x, adj, L1_gnn_W, L1_gnn_b, L1_gnn_a_s, L1_gnn_a_r), axis=-1)
    return x

_drawn_inputs = setup_inputs


def setup_inputs(seed=0):
    import zlib

    import numpy as np

    out = dict(_drawn_inputs(seed))
    spreads = {'L1_gnn_b': (0.0, 0.1)}
    factors = {}
    for name, (base, spread) in spreads.items():
        noise = np.random.default_rng([zlib.crc32(name.encode()), seed]).standard_normal(out[name].shape)
        drawn = base * np.exp(spread * noise) if base else spread * noise
        out[name] = jnp.asarray(drawn.astype(out[name].dtype))
    for name, factor in factors.items():
        out[name] = (out[name] * factor).astype(out[name].dtype)
    return out
```

```python
from contextlib import ExitStack

import concourse.bass as bass
from concourse import mybir

P = 128
BANK = 512
ALU = mybir.AluOpType
ACT = mybir.ActivationFunctionType
F32 = mybir.dt.float32
F32R = mybir.dt.float32r
BF16 = mybir.dt.bfloat16

MIX = 0.1
SLOPE = 0.2
EPS = 1e-5
LEAST_SHIFT = 1.0
MASKED_BY = 2.0 ** 14


def gnn_kernel(nc, x, adj, h, W, b, a_s, a_r, out):
    N, F = x.shape
    D = W.shape[0]
    assert F == P and D == P and N % 4096 == 0
    NB = N // P

    SUB = BANK // P
    GROUPS = N // BANK
    JW = 512
    LOADS = N // JW
    BPL = JW // P
    RING = 4
    TB = 4
    LAG = 3
    XPIECE = 1024
    XPIECES = N // XPIECE
    XLOADS = XPIECE // JW
    XBLOCKS = XPIECE // P

    TILES = NB
    CW = N // 4
    CHUNKS = N // CW
    QB = 2 * BANK // P
    QPC = CW // (QB * P)
    QPT = CHUNKS * QPC
    AHEAD = 2
    PLAIN = CHUNKS - 1
    SIGNED = PLAIN - 1
    SIGNS_AT, SQUARES_AT = QPC, 2 * QPC
    ROOT = MASKED_BY ** -0.5
    HC = D + 2

    scratch = nc.dram_tensor("x1_scratch", (N, F), F32, kind="Internal").ap()

    adj_groups = adj.rearrange("(g a p) j -> g p a j", a=SUB, p=P)
    adj_tiles = adj.rearrange("(t p) j -> t p j", p=P)
    x_groups = x.rearrange("(g a p) f -> g p a f", a=SUB, p=P)
    h_groups = h.rearrange("(g a p) f -> g p a f", a=SUB, p=P)
    x1_groups = scratch.rearrange("(g a p) f -> g p a f", a=SUB, p=P)
    x1_tiles = scratch.rearrange("(t p) f -> t p f", p=P)
    out_tiles = out.rearrange("(t p) f -> t p f", p=P)

    with ExitStack() as ctx:
        def sem(name):
            return ctx.enter_context(nc.semaphore(name))

        def sb(name, shape, dt=F32, scope=ctx):
            return scope.enter_context(nc.sbuf_tensor(name, shape, dt))

        ps = ctx.enter_context(nc.psum_tensor("ps", [P, 8, BANK], F32))

        ident = sb("ident", [P, P])
        bias = sb("bias", [P, 1])
        att = sb("att", [P, 2])
        power = sb("power", [P, SUB])
        s_cols = sb("s_cols", [P, NB])
        leak_cols = sb("leak_cols", [P, NB])
        r_wide = sb("r_wide", [P, N])
        ones_col = sb("ones_col", [P, 1])
        Haug = sb("Haug", [P, NB, HC])
        a_ring = sb("a_ring", [P, RING * SUB * JW])

        one = ones_col[:, 0:1]
        load_slot = a_ring[:, :].rearrange("p (s a j) -> p s a j", s=RING, a=SUB)
        chunk_slot = a_ring[:, 0:RING * CW].rearrange("p (s j) -> p s j", s=RING)
        x_raw = Haug[:, :, :].rearrange("p b c -> p (b c)")[:, 0:N]

        const_in = sem("const_in")
        x_in = [sem(f"x_in{i}") for i in range(XPIECES)]
        ident_done = sem("ident_done")
        const_done = sem("const_done")
        slot_in = [sem(f"slot_in{i}") for i in range(RING)]
        chunk_in = [sem(f"chunk_in{i}") for i in range(RING)]
        wt_turned = sem("wt_turned")
        wt_done = sem("wt_done")
        xh_done = sem("xh_done")
        xl_done = sem("xl_done")
        turned = sem("turned")
        hi_done = sem("hi_done")
        lo_done = sem("lo_done")
        multiplied = sem("multiplied")
        prod_moved = sem("prod_moved")
        prod_turned = sem("prod_turned")
        xg_in = sem("xg_in")
        hg_in = sem("hg_in")
        vchain = sem("vchain")
        stats_done = sem("stats_done")
        gpow = sem("gpow")
        rstd_done = sem("rstd_done")
        xh_rows_used = sem("xh_rows_used")
        x1_done = sem("x1_done")
        x1_out = sem("x1_out")
        x1_turned = sem("x1_turned")
        x1t_moved = sem("x1t_moved")
        proj_done = sem("proj_done")
        ht_moved = sem("ht_moved")
        heads_done = sem("heads_done")
        r_moved = sem("r_moved")
        sh_moved = sem("sh_moved")

        def wait(eng, s, value):
            if not isinstance(value, int) or value > 0:
                eng.wait_ge(s, value)

        def wait_apart(eng, *waits):
            if all(isinstance(value, int) for _, value in waits):
                for s, value in waits:
                    wait(eng, s, value)
            else:
                held = [(s, eng.to_reg(value)) for s, value in waits]
                eng.wait_ge(const_in, 64)
                for s, value in held:
                    eng.wait_ge(s, value)

        L0 = ExitStack()
        with L0:
            Wn = sb("Wn", [P, F], F32, L0)
            WT = sb("WT", [P, D], F32, L0)
            ones = sb("ones", [P, P], F32, L0)
            ar_wide = sb("ar_wide", [P, P], F32, L0)
            xh = sb("xh", [P, N], F32R, L0)
            xl = sb("xl", [P, N], F32R, L0)
            ah = sb("ah", [P, TB, BANK], F32R, L0)
            al = sb("al", [P, TB, BANK], F32R, L0)
            xg = sb("xg", [P, BANK], F32, L0)
            hg = sb("hg", [P, BANK], F32, L0)
            xhg = sb("xhg", [P, BANK], F32, L0)
            prod = sb("prod", [P, BANK], F32, L0)
            y0 = sb("y0", [P, SUB, F], F32, L0)
            x1 = sb("x1", [P, SUB, F], F32, L0)
            x1T = sb("x1T", [P, BANK], F32, L0)
            HT = sb("HT", [P, BANK], F32, L0)
            st0 = sb("st0", [P, SUB, 6], F32, L0)
            mv0 = sb("mv0", [P, SUB, 2], F32, L0)
            ve0 = sb("ve0", [P, SUB], F32, L0)
            rstd0 = sb("rstd0", [P, SUB], F32, L0)

            PROD, M0, M1, M2 = TB, TB + 1, TB + 2, TB + 3

            at = {name: k * NB // 64 for name, k in dict(
                move=2, turn=5, rows=7, norm=16, x1t=20, x1tm=22, proj=24, projm=27, heads=30, headm=33).items()}

            block = L0.enter_context(nc.Block())

            @block.sync
            def _(sp):
                sp.dma_start(Wn[:, :], W).then_inc(const_in, 16)
                sp.dma_start(bias[:, :], b.rearrange("(d one) -> d one", one=1)).then_inc(const_in, 16)
                sp.dma_start(att[:, 0:1], a_s).then_inc(const_in, 16)
                sp.dma_start(att[:, 1:2], a_r).then_inc(const_in, 16)
                xv = x.rearrange("(b p) f -> p b f", p=P)
                BX = XPIECE // F

                def loads(g):
                    for c in range(LOADS):
                        if isinstance(g, int) and g == 0 and c % XLOADS == 0:
                            i = c // XLOADS
                            sp.dma_start(x_raw[:, i * XPIECE:(i + 1) * XPIECE].rearrange("p (b f) -> p b f", f=F),
                                         xv[:, i * BX:(i + 1) * BX, :]).then_inc(x_in[i], 16)
                        wait(sp, turned, (g * LOADS + c - RING + 1) * BPL)
                        sp.dma_start(load_slot[:, c % RING], adj_groups[g, :, :, c * JW:(c + 1) * JW])\
                            .then_inc(slot_in[c % RING], 16)
                loads(0)
                with sp.Fori(1, GROUPS) as g:
                    loads(g)
                for c in range(RING):
                    wait(sp, turned, (GROUPS * LOADS - RING + c + 1) * BPL)
                    sp.dma_start(chunk_slot[:, c], adj_tiles[0, :, c * CW:(c + 1) * CW]).then_inc(chunk_in[c], 16)

            @block.gpsimd
            def _(pool):
                pool.memset(ones[:, :], 1.0).then_inc(ident_done, 1)
                pool.wait_ge(ident_done, 1)
                pool.affine_select(out=ident[:, :], in_=ones[:, :], compare_op=ALU.is_equal, fill=0.0,
                                   base=0, pattern=[[-1, P]], channel_multiplier=1).then_inc(ident_done, 1)
                pool.memset(ones_col[:, :], 1.0)
                pool.memset(power[:, :], -0.5).then_inc(ident_done, 1)

                def rows_in(g):
                    wait(pool, xh_rows_used, g)
                    pool.dma_start(xg[:, :].rearrange("p (a f) -> p a f", a=SUB), x_groups[g]).then_inc(xg_in, 16)
                    pool.dma_start(hg[:, :].rearrange("p (a f) -> p a f", a=SUB), h_groups[g]).then_inc(hg_in, 16)

                def norm_and_store(g):
                    wait_apart(pool, (stats_done, g + 1))
                    pool.tensor_scalar(ve0[:, :], mv0[:, :, 1], EPS, None, ALU.add).then_inc(gpow, 1)
                    pool.wait_ge(gpow, g + 1)
                    pool.tensor_tensor(rstd0[:, :], ve0[:, :], power[:, :], ALU.pow).then_inc(rstd_done, 1)
                    pool.wait_ge(x1_done, g + 1)
                    pool.dma_start(x1_groups[g], x1[:, :, :]).then_inc(x1_out, 16)

                pool.wait_ge(ident_done, 3)
                rows_in(0)
                with pool.Fori(1, GROUPS) as g:
                    rows_in(g)
                    norm_and_store(g - 1)
                norm_and_store(GROUPS - 1)
                pool.wait_ge(x1_out, 16 * GROUPS)

            @block.scalar
            def _(act):
                def x_hi(i):
                    act.wait_ge(x_in[i], 16)
                    cols = slice(i * XPIECE, (i + 1) * XPIECE)
                    act.copy(xh[:, cols], x_raw[:, cols]).then_inc(xh_done, 1)

                x_hi(0)
                act.wait_ge(wt_turned, 1)
                act.copy(WT[:, :], ps[:, M0, 0:D]).then_inc(wt_done, 1)

                def hi(g, k):
                    n = g * NB + k
                    act.wait_ge(turned, n + 1)
                    wait(act, multiplied, n - TB + 1)
                    act.copy(ah[:, k % TB], ps[:, k % TB]).then_inc(hi_done, 1)

                def move(g):
                    act.wait_ge(multiplied, (g + 1) * NB)
                    wait(act, prod_turned, g)
                    act.mul(prod[:, :], ps[:, PROD], 1.0 - MIX).then_inc(prod_moved, 1)

                def move_x1t(g):
                    act.wait_ge(x1_turned, g + 1)
                    act.copy(x1T[:, :], ps[:, M1]).then_inc(x1t_moved, 1)

                def move_ht(g):
                    act.wait_ge(proj_done, g + 1)
                    act.activation(HT[:, :], ps[:, M0], ACT.Identity, bias=bias[:, 0:1]).then_inc(ht_moved, 1)

                def move_r(g):
                    act.wait_ge(heads_done, g + 1)
                    act.copy(r_wide[:, bass.ds(g * BANK, BANK)], ps[:, M1]).then_inc(r_moved, 1)

                def group(g, before):
                    for k in range(NB):
                        hi(g, k)
                        if before is None and k % XBLOCKS == XBLOCKS // 2 and k // XBLOCKS + 1 < XPIECES:
                            x_hi(k // XBLOCKS + 1)
                        if before is not None:
                            if k == at["move"]:
                                move(before)
                            if k == at["x1tm"]:
                                move_x1t(before)
                            if k == at["projm"]:
                                move_ht(before)
                            if k == at["headm"]:
                                move_r(before)
                group(0, None)
                with act.Fori(1, GROUPS) as g:
                    group(g, g - 1)
                for stage in (move, move_x1t, move_ht, move_r):
                    stage(GROUPS - 1)

            @block.vector
            def _(dve):
                dve.wait_ge(const_in, 64)
                dve.wait_ge(ident_done, 3)
                dve.tensor_scalar(ar_wide[:, :], ones[:, :], att[:, 1:2], None, ALU.mult).then_inc(const_done, 1)

                def x_lo(i):
                    dve.wait_ge(xh_done, i + 1)
                    cols = slice(i * XPIECE, (i + 1) * XPIECE)
                    dve.tensor_tensor(xl[:, cols], x_raw[:, cols], xh[:, cols], ALU.subtract).then_inc(xl_done, 1)

                x_lo(0)

                def lo(g, k):
                    dve.wait_ge(hi_done, g * NB + k + 1)
                    dve.tensor_tensor(al[:, k % TB], ps[:, k % TB], ah[:, k % TB], ALU.subtract).then_inc(lo_done, 1)

                def rows(g):
                    dve.wait_ge(xg_in, 16 * (g + 1))
                    dve.wait_ge(hg_in, 16 * (g + 1))
                    dve.scalar_tensor_tensor(out=xhg[:, :], in0=hg[:, :], scalar=MIX, in1=xg[:, :],
                                             op0=ALU.mult, op1=ALU.add).then_inc(xh_rows_used, 1)
                    dve.wait_ge(xh_rows_used, g + 1)
                    dve.wait_ge(prod_turned, g + 1)
                    dve.tensor_tensor(y0[:, :, :].rearrange("p a f -> p (a f)"), ps[:, M0], xhg[:, :], ALU.add)\
                        .then_inc(vchain, 1)
                    dve.wait_ge(vchain, g * (1 + SUB) + 1)
                    for a in range(SUB):
                        dve.bn_stats(st0[:, a, :], y0[:, a, :]).then_inc(vchain, 1)
                    wait_apart(dve, (vchain, (g + 1) * (1 + SUB)))
                    for a in range(SUB):
                        last = dve.bn_aggr(mv0[:, a, :], st0[:, a, :])
                    last.then_inc(stats_done, 1)

                def norm(g):
                    dve.wait_ge(rstd_done, g + 1)
                    wait(dve, x1_out, 16 * g)
                    for a in range(SUB):
                        last = dve.tensor_scalar(x1[:, a, :], y0[:, a, :], mv0[:, a, 0:1], rstd0[:, a:a + 1],
                                                 ALU.subtract, ALU.mult)
                    last.then_inc(x1_done, 1)

                def move_sh(g):
                    dve.wait_ge(heads_done, g + 1)
                    dve.tensor_copy(Haug[:, bass.ds(g * SUB, SUB), 0:D],
                                    ps[:, M0].rearrange("p (a d) -> p a d", a=SUB))
                    dve.tensor_copy(s_cols[:, bass.ds(g * SUB, SUB)], ps[:, M2, 0:SUB])
                    dve.tensor_scalar(leak_cols[:, bass.ds(g * SUB, SUB)], ps[:, M2, 0:SUB], SLOPE, None, ALU.mult)\
                        .then_inc(sh_moved, 1)

                def group(g, before):
                    for k in range(NB):
                        lo(g, k)
                        if before is None and k % XBLOCKS == XBLOCKS // 2 and k // XBLOCKS + 1 < XPIECES:
                            x_lo(k // XBLOCKS + 1)
                        if before is not None:
                            if k == at["rows"]:
                                rows(before)
                            if k == at["norm"]:
                                norm(before)
                            if k == at["headm"]:
                                move_sh(before)
                group(0, None)
                dve.wait_ge(xl_done, XPIECES)
                dve.memset(Haug[:, :, D:HC], 1.0).then_inc(const_done, 1)
                with dve.Fori(1, GROUPS) as g:
                    group(g, g - 1)
                for stage in (rows, norm, move_sh):
                    stage(GROUPS - 1)

            @block.tensor
            def _(pe):
                pe.wait_ge(const_in, 64)
                pe.wait_ge(ident_done, 3)
                pe.transpose(ps[:, M0, 0:D], Wn[:, :], ident[:, :]).then_inc(wt_turned, 1)

                def turn(g, k):
                    n = g * NB + k
                    if k % BPL == 0:
                        c = k // BPL
                        pe.wait_ge(slot_in[c % RING], 16 * ((LOADS // RING) * g + c // RING + 1))
                    wait(pe, lo_done, n - TB + 1)
                    for a in range(SUB):
                        j = (k % BPL) * P
                        last = pe.transpose(ps[:, k % TB, a * P:(a + 1) * P],
                                            load_slot[:, (k // BPL) % RING, a, j:j + P], ident[:, :])
                    last.then_inc(turned, 1)

                def multiply(g, k):
                    pe.wait_ge(lo_done, g * NB + k + 1)
                    if isinstance(g, int) and g == 0 and k % XBLOCKS == 0:
                        pe.wait_ge(xl_done, k // XBLOCKS + 1)
                    if k == 0:
                        wait(pe, prod_moved, g)
                    cols = slice(k * P, (k + 1) * P)
                    pe.matmul(ps[:, PROD], xh[:, cols], ah[:, k % TB], start=(k == 0), stop=False)
                    pe.matmul(ps[:, PROD], xl[:, cols], ah[:, k % TB], start=False, stop=False)
                    pe.matmul(ps[:, PROD], xh[:, cols], al[:, k % TB], start=False, stop=(k == NB - 1))\
                        .then_inc(multiplied, 1)

                def turn_prod(g):
                    pe.wait_ge(prod_moved, g + 1)
                    wait(pe, sh_moved, g)
                    if isinstance(g, int) and g == 0:
                        pe.wait_ge(wt_done, 1)
                    for a in range(SUB):
                        last = pe.transpose(ps[:, M0, a * P:(a + 1) * P], prod[:, a * P:(a + 1) * P], ident[:, :])
                    last.then_inc(prod_turned, 1)

                def turn_x1(g):
                    pe.wait_ge(x1_done, g + 1)
                    wait(pe, r_moved, g)
                    for a in range(SUB):
                        last = pe.transpose(ps[:, M1, a * P:(a + 1) * P], x1[:, a, :], ident[:, :])
                    last.then_inc(x1_turned, 1)

                def project(g):
                    pe.wait_ge(x1t_moved, g + 1)
                    pe.wait_ge(wt_done, 1)
                    pe.matmul(ps[:, M0], WT[:, :], x1T[:, :], start=True, stop=True).then_inc(proj_done, 1)

                def heads(g):
                    pe.wait_ge(ht_moved, g + 1)
                    pe.wait_ge(const_done, 2)
                    pe.matmul(ps[:, M1], ar_wide[:, :], HT[:, :], start=True, stop=True)
                    for a in range(SUB):
                        pe.matmul(ps[:, M2, a:a + 1], HT[:, a * P:(a + 1) * P], att[:, 0:1], start=True, stop=True)
                    for a in range(SUB):
                        last = pe.transpose(ps[:, M0, a * P:(a + 1) * P], HT[:, a * P:(a + 1) * P], ident[:, :])
                    last.then_inc(heads_done, 1)

                def group(g, before):
                    for k in range(NB):
                        turn(g, k)
                        if k >= LAG:
                            multiply(g, k - LAG)
                        elif before is not None:
                            multiply(before, NB - LAG + k)
                        if before is not None:
                            if k == at["turn"]:
                                turn_prod(before)
                            if k == at["x1t"]:
                                turn_x1(before)
                            if k == at["proj"]:
                                project(before)
                            if k == at["heads"]:
                                heads(before)
                group(0, None)
                with pe.Fori(1, GROUPS) as g:
                    group(g, g - 1)
                for k in range(NB - LAG, NB):
                    multiply(GROUPS - 1, k)
                for stage in (turn_prod, turn_x1, project, heads):
                    stage(GROUPS - 1)

        leak_done = sem("leak_done")
        leaky_done = sem("leaky_done")
        edges_done = sem("edges_done")
        sign_done = sem("sign_done")
        signed_done = sem("signed_done")
        logits_done = sem("logits_done")
        shift_done = sem("shift_done")
        col_done = sem("col_done")
        bias_done = sem("bias_done")
        plain_exp = sem("plain_exp")
        plain_done = sem("plain_done")
        p_turned = sem("p_turned")
        exp_done = sem("exp_done")
        q_used = sem("q_used")
        x1r_in = [sem(f"x1r_in{i}") for i in range(2)]
        recip_done = sem("recip_done")
        res_done = sem("res_done")
        st_done = sem("st_done")
        mv_done = sem("mv_done")
        eps_done = sem("eps_done")
        rs_done = sem("rs_done")
        normed = sem("normed")
        stored = [sem(f"stored{i}") for i in range(2)]

        L1 = ExitStack()
        with L1:
            t = [sb(f"t{i}", [P, N], F32, L1) for i in range(2)]
            edge = [sb(f"edge{i}", [P, PLAIN * CW], BF16, L1) for i in range(2)]
            pt = sb("pt", [P, 2, QB * P], F32, L1)
            x1r = sb("x1r", [P, 2, F], F32, L1)
            y1 = sb("y1", [P, 2, F], F32, L1)
            o1 = sb("o1", [P, 2, F], F32, L1)
            high = sb("high", [P, 2, CHUNKS], F32, L1)
            shift = sb("shift", [P, 2, P], BF16, L1)
            shift_col = sb("shift_col", [P, 2], BF16, L1)
            shift_bias = sb("shift_bias", [P, 2], F32, L1)
            rden = sb("rden", [P, 2], F32, L1)
            st1 = sb("st1", [P, 2, 6], F32, L1)
            mv1 = sb("mv1", [P, 2, 2], F32, L1)
            ve1 = sb("ve1", [P, 2], F32, L1)
            rstd1 = sb("rstd1", [P, 2], F32, L1)

            quota_ps = ps[:, 0:4, :].rearrange("p (q b) n -> p q (b n)", q=2)
            OUT = 4

            block = L1.enter_context(nc.Block())

            def steps(eng, step):
                for e in range(2):
                    step(e, e)
                with eng.Fori(1, TILES // 2 - 1) as u:
                    for e in range(2):
                        step(2 * u + e, e)
                for e in range(2):
                    step(TILES - 2 + e, e)

            def before(i, e):
                return i // 2 if isinstance(i, int) else (i - e) // 2

            def is_first(i):
                return isinstance(i, int) and i == 0

            def is_last(i):
                return isinstance(i, int) and i == TILES - 1

            def chunk(c):
                return slice(c * CW, (c + 1) * CW)

            @block.sync
            def _(sp):
                def load(i):
                    for c in range(CHUNKS):
                        if c == PLAIN:
                            sp.wait_ge(plain_done, i)
                        else:
                            read = sp.to_reg((i - 1) * CHUNKS + c + 1)
                            if c == SIGNED:
                                sp.wait_ge(sign_done, i)
                            sp.wait_ge(logits_done, read)
                        sp.dma_start(chunk_slot[:, c], adj_tiles[i, :, chunk(c)]).then_inc(chunk_in[c], 16)
                with sp.Fori(1, TILES) as i:
                    load(i)

            @block.gpsimd
            def _(pool):
                def x1_in(i, e):
                    pool.dma_start(x1r[:, e, :], x1_tiles[i]).then_inc(x1r_in[e], 16)

                x1_in(0, 0)
                x1_in(1, 1)

                def finish(i, e):
                    wait_apart(pool, (mv_done, i + 1))
                    pool.tensor_scalar(ve1[:, e:e + 1], mv1[:, e, 1:2], EPS, None, ALU.add).then_inc(eps_done, 1)
                    if not (isinstance(i, int) and i >= TILES - 2):
                        x1_in(i + 2, e)
                    pool.wait_ge(eps_done, i + 1)
                    pool.tensor_tensor(rstd1[:, e:e + 1], ve1[:, e:e + 1], power[:, 0:1], ALU.pow).then_inc(rs_done, 1)
                    wait_apart(pool, (rs_done, i + 1), (stored[e], 16 * before(i, e)))
                    pool.tensor_scalar(o1[:, e, :], y1[:, e, :], mv1[:, e, 0:1], rstd1[:, e:e + 1],
                                       ALU.subtract, ALU.mult).then_inc(normed, 1)
                    pool.wait_ge(normed, i + 1)
                    pool.dma_start(out_tiles[i], o1[:, e, :]).then_inc(stored[e], 16)
                steps(pool, finish)
                for e in range(2):
                    pool.wait_ge(stored[e], 16 * (TILES // 2))

            @block.scalar
            def _(act):
                def leak(i, e, c):
                    wait_apart(act, (p_turned, (i - 2) * QPT + (c + 1) * QPC))
                    act.activation(t[e][:, chunk(c)], r_wide[:, chunk(c)], ACT.Identity, scale=SLOPE,
                                   bias=leak_cols[:, bass.ds(i, 1)]).then_inc(leak_done, 1)

                def probabilities(i, q):
                    act.wait_ge(p_turned, i * QPT + q + 1)
                    wait(act, q_used, i * QPT + q - 1)
                    if q // QPC == PLAIN:
                        act.copy(pt[:, q % 2], quota_ps[:, q % 2]).then_inc(exp_done, 1)
                    else:
                        act.activation(pt[:, q % 2], quota_ps[:, q % 2], ACT.Exp).then_inc(exp_done, 1)

                def signs(i, e):
                    wait(act, p_turned, (i - 2) * QPT + (SIGNED + 1) * QPC)
                    act.wait_ge(chunk_in[SIGNED], 16 * (i + 1))
                    act.activation(edge[e][:, chunk(SIGNED)], chunk_slot[:, SIGNED], ACT.Sign).then_inc(sign_done, 1)

                def squares(i, e):
                    act.wait_ge(sign_done, i + 1)
                    act.activation(edge[e][:, chunk(SIGNED)], edge[e][:, chunk(SIGNED)], ACT.Square,
                                   scale=ROOT - 1.0, bias=one).then_inc(signed_done, 1)

                def plain(i, e):
                    act.wait_ge(bias_done, i + 1)
                    act.activation(t[e][:, chunk(PLAIN)], t[e][:, chunk(PLAIN)], ACT.Exp,
                                   bias=shift_bias[:, e:e + 1]).then_inc(plain_exp, 1)

                for c in range(CHUNKS):
                    leak(0, 0, c)
                for c in range(AHEAD):
                    leak(1, 1, c)
                signs(0, 0)
                squares(0, 0)

                def step(i, e):
                    for c in range(CHUNKS):
                        for q in range(c * QPC, (c + 1) * QPC):
                            probabilities(i, q)
                            if q == 0:
                                plain(i, e)
                            if q == SIGNS_AT and not is_last(i):
                                signs(i + 1, 1 - e)
                            if q == SQUARES_AT and not is_last(i):
                                squares(i + 1, 1 - e)
                        if c + AHEAD < CHUNKS:
                            if not is_last(i):
                                leak(i + 1, 1 - e, c + AHEAD)
                        elif not (isinstance(i, int) and i >= TILES - 2):
                            leak(i + 2, e, c + AHEAD - CHUNKS)
                steps(act, step)

            @block.vector
            def _(dve):
                def logits(i, e, c):
                    dve.wait_ge(leak_done, i * CHUNKS + c + 1)
                    dve.scalar_tensor_tensor(out=t[e][:, chunk(c)], in0=r_wide[:, chunk(c)],
                                             scalar=s_cols[:, bass.ds(i, 1)], in1=t[e][:, chunk(c)],
                                             op0=ALU.add, op1=ALU.max).then_inc(leaky_done, 1)
                    landed = [(chunk_in[c], 16 * (i + 1))]
                    if c not in (PLAIN, SIGNED):
                        dve.wait_ge(*landed.pop())
                        wait(dve, p_turned, (i - 2) * QPT + (c + 1) * QPC)
                        dve.tensor_scalar(edge[e][:, chunk(c)], chunk_slot[:, c], 0.0, 1.0 / MASKED_BY,
                                          ALU.is_le, ALU.add).then_inc(edges_done, 1)
                    so_far = [(logits_done, i * CHUNKS + c)] if c > 0 else []
                    wait_apart(dve, (leaky_done, i * CHUNKS + c + 1), *so_far, *landed)
                    dve.tensor_tensor_reduce(out=t[e][:, chunk(c)], in0=chunk_slot[:, c], in1=t[e][:, chunk(c)],
                                             scale=1.0, scalar=LEAST_SHIFT if c == 0 else high[:, e, c - 1:c],
                                             op0=ALU.mult, op1=ALU.max,
                                             accum_out=high[:, e, c:c + 1]).then_inc(logits_done, 1)
                    if c == CHUNKS - 1:
                        dve.wait_ge(logits_done, (i + 1) * CHUNKS)
                        dve.tensor_scalar(shift[:, e, :], ident[:, :], high[:, e, c:c + 1], -MASKED_BY,
                                          ALU.mult, ALU.mult).then_inc(shift_done, 1)
                        dve.tensor_scalar(shift_col[:, e:e + 1], high[:, e, c:c + 1], -MASKED_BY, None, ALU.mult)\
                            .then_inc(col_done, 1)
                        dve.wait_ge(col_done, i + 1)
                        dve.tensor_scalar(shift_bias[:, e:e + 1], shift_col[:, e:e + 1], 1.0 / MASKED_BY, None,
                                          ALU.mult).then_inc(bias_done, 1)

                def mask(i, e):
                    dve.wait_ge(plain_exp, i + 1)
                    dve.scalar_tensor_tensor(out=t[e][:, chunk(PLAIN)], in0=chunk_slot[:, PLAIN], scalar=0.0,
                                             in1=t[e][:, chunk(PLAIN)], op0=ALU.is_gt, op1=ALU.mult)\
                        .then_inc(plain_done, 1)

                def rows(i, e):
                    dve.wait_ge(q_used, (i + 1) * QPT)
                    dve.reciprocal(rden[:, e:e + 1], ps[:, OUT + e, D:D + 1]).then_inc(recip_done, 1)
                    dve.wait_ge(recip_done, i + 1)
                    dve.wait_ge(x1r_in[e], 16 * (before(i, e) + 1))
                    wait(dve, normed, i - 1)
                    dve.scalar_tensor_tensor(out=y1[:, e, :], in0=ps[:, OUT + e, 0:D], scalar=rden[:, e:e + 1],
                                             in1=x1r[:, e, :], op0=ALU.mult, op1=ALU.add).then_inc(res_done, 1)
                    dve.wait_ge(res_done, i + 1)
                    dve.bn_stats(st1[:, e, :], y1[:, e, :]).then_inc(st_done, 1)
                    wait_apart(dve, (st_done, i + 1))
                    dve.bn_aggr(mv1[:, e, :], st1[:, e, :]).then_inc(mv_done, 1)

                for c in range(CHUNKS):
                    logits(0, 0, c)

                def step(i, e):
                    for c in range(CHUNKS):
                        if not is_last(i):
                            logits(i + 1, 1 - e, c)
                        if c == 0:
                            mask(i, e)
                        if c == 1 and not is_first(i):
                            rows(i - 1, 1 - e)
                steps(dve, step)
                rows(TILES - 1, 1)

            @block.tensor
            def _(pe):
                def turn(i, e, q):
                    if q == 0:
                        pe.wait_ge(shift_done, i + 1)
                    if q == SIGNED * QPC:
                        pe.wait_ge(signed_done, i + 1)
                    wait(pe, exp_done, i * QPT + q - 1)
                    if q == PLAIN * QPC:
                        pe.wait_ge(plain_done, i + 1)
                    for n in range(QB):
                        col = (q * QB + n) * P
                        to = quota_ps[:, q % 2, n * P:(n + 1) * P]
                        if q // QPC == PLAIN:
                            last = pe.transpose(to, t[e][:, col:col + P], ident[:, :])
                            continue
                        pe.matmul(to, t[e][:, col:col + P], ident[:, :], is_transpose=True, start=True, stop=False)
                        last = pe.matmul(to, edge[e][:, col:col + P], shift[:, e, :], start=False, stop=True)
                    last.then_inc(p_turned, 1)

                def multiply(i, e, q):
                    pe.wait_ge(exp_done, i * QPT + q + 1)
                    if q == 0:
                        wait(pe, res_done, i - 1)
                    for n in range(QB):
                        blk = q * QB + n
                        last = pe.matmul(ps[:, OUT + e, 0:HC], pt[:, q % 2, n * P:(n + 1) * P], Haug[:, blk, :],
                                         start=(blk == 0), stop=(blk == NB - 1))
                    last.then_inc(q_used, 1)

                def step(i, e):
                    for q in range(QPT):
                        turn(i, e, q)
                        if q > 0:
                            multiply(i, e, q - 1)
                        elif not is_first(i):
                            multiply(i - 1, 1 - e, QPT - 1)
                steps(pe, step)
                multiply(TILES - 1, 1, QPT - 1)


_INS = ['x', 'adj', 'L0_gnn_h', 'L1_gnn_W', 'L1_gnn_b', 'L1_gnn_a_s', 'L1_gnn_a_r']


def kernel(**inputs):
    import numpy as _np
    import concourse.bacc as _bacc
    from concourse import mybir as _mybir
    from concourse.bass_utils import run_bass_kernel_spmd as _run

    nc = _bacc.Bacc("TRN2", target_bir_lowering=False, num_devices=1)
    arrays, args = {}, []
    for name in _INS:
        a = _np.ascontiguousarray(inputs[name])
        arrays[f"in_{name}"] = a
        args.append(nc.dram_tensor(f"in_{name}", a.shape, _mybir.dt.from_np(a.dtype), kind="ExternalInput").ap())
    args.append(nc.dram_tensor("out_x", inputs["x"].shape, _mybir.dt.float32, kind="ExternalOutput").ap())
    gnn_kernel(nc, *args)
    r = _run(nc, [arrays], core_ids=[0])
    return r.results[0]["out_x"]
```

```python
from contextlib import ExitStack

import concourse.bass as bass
from concourse import mybir

P = 128
BANK = 512
ALU = mybir.AluOpType
ACT = mybir.ActivationFunctionType
F32 = mybir.dt.float32
F32R = mybir.dt.float32r
BF16 = mybir.dt.bfloat16

MIX = 0.1
SLOPE = 0.2
EPS = 1e-5
LEAST_SHIFT = 1.0
MASKED_BY = 2.0 ** 14


def gnn_kernel(nc, x, adj, h, W, b, a_s, a_r, out):
    N, F = x.shape
    D = W.shape[0]
    assert F == P and D == P and N % 4096 == 0
    NB = N // P

    SUB = BANK // P
    GROUPS = N // BANK
    JW = 512
    LOADS = N // JW
    BPL = JW // P
    RING = 4
    TB = 5
    TURN_BANKS = 4
    LAG = 4
    V_LOADS = 2 * (3 * LOADS // 16)
    T_LOADS = LOADS - V_LOADS
    V_BLOCKS, T_BLOCKS = V_LOADS * BPL, T_LOADS * BPL
    kinds = ["V" if ((k + 1) * V_BLOCKS + NB // 2) // NB > (k * V_BLOCKS + NB // 2) // NB else "T" for k in range(NB)]
    nth = [kinds[:k].count(kinds[k]) for k in range(NB)]
    step_of = {kind: [k for k in range(NB) if kinds[k] == kind] for kind in "TV"}
    x_block = [nth[k] + (T_BLOCKS if kinds[k] == "V" else 0) for k in range(NB)]
    load_order = sorted(((kind, c) for kind, loads in (("T", T_LOADS), ("V", V_LOADS)) for c in range(loads)),
                        key=lambda load: step_of[load[0]][load[1] * BPL])
    VLEAD = 2
    XBEFORE = 5
    XPIECE = 1024
    XBLOCKS = XPIECE // P
    XPIECES = N // XPIECE
    first_step = [min(k for k in range(NB) if x_block[k] // XBLOCKS == i) for i in range(XPIECES)]
    piece_order = sorted(range(XPIECES), key=lambda i: first_step[i])
    Q = 32
    assert V_LOADS % 2 == 0 and T_LOADS % 2 == 0 and T_BLOCKS % XBLOCKS == 0

    TILES = NB
    TURNS = 4
    assert (TILES - 4) % TURNS == 0
    CW = N // 4
    CHUNKS = N // CW
    QB = 2 * BANK // P
    QPC = CW // (QB * P)
    QPT = CHUNKS * QPC
    AHEAD = 2
    PLAIN = CHUNKS - 1
    SIGNED = PLAIN - 1
    SIGNS_AT, SQUARES_AT = QPC, 2 * QPC
    ROOT = MASKED_BY ** -0.5
    HC = D + 1

    scratch = nc.dram_tensor("x1_scratch", (N, F), F32, kind="Internal").ap()

    adj_groups = adj.rearrange("(g a p) j -> g p a j", a=SUB, p=P)
    adj_tiles = adj.rearrange("(t p) j -> t p j", p=P)
    adj_squares = adj.rearrange("(g m r) (l q w) -> g l q r m w", m=BANK // Q, r=Q, q=P // Q, w=P)
    x_squares = x.rearrange("(l q s r) f -> l q r s f", q=P // Q, s=JW // P, r=Q)
    x_groups = x.rearrange("(g a p) f -> g p a f", a=SUB, p=P)
    h_groups = h.rearrange("(g a p) f -> g p a f", a=SUB, p=P)
    x1_groups = scratch.rearrange("(g a p) f -> g p a f", a=SUB, p=P)
    x1_tiles = scratch.rearrange("(t p) f -> t p f", p=P)
    out_tiles = out.rearrange("(t p) f -> t p f", p=P)

    with ExitStack() as ctx:
        def sem(name):
            return ctx.enter_context(nc.semaphore(name))

        def sb(name, shape, dt=F32, scope=ctx):
            return scope.enter_context(nc.sbuf_tensor(name, shape, dt))

        ps = ctx.enter_context(nc.psum_tensor("ps", [P, 8, BANK], F32))

        ident = sb("ident", [P, P])
        bias = sb("bias", [P, 1])
        att = sb("att", [P, 2])
        power = sb("power", [P, SUB])
        sr_cols = sb("sr_cols", [P, NB, 2])
        leak_cols = sb("leak_cols", [P, NB])
        r_wide = sb("r_wide", [P, N])
        ones_col = sb("ones_col", [P, 1])
        Haug = sb("Haug", [P, NB, HC])
        a_ring = sb("a_ring", [P, RING * SUB * JW])

        one = ones_col[:, 0:1]
        square_slot = a_ring[:, :].rearrange("p (s m w) -> p s m w", s=RING, m=BANK // Q)
        load_slot = a_ring[:, :].rearrange("p (s a j) -> p s a j", s=RING, a=SUB)
        chunk_slot = a_ring[:, 0:RING * CW].rearrange("p (s j) -> p s j", s=RING)
        x_raw = Haug[:, :, :].rearrange("p b c -> p (b c)")[:, 0:N]

        const_in = sem("const_in")
        x_in = [sem(f"x_in{i}") for i in range(XPIECES)]
        ident_done = sem("ident_done")
        const_done = sem("const_done")
        slot_in = [sem(f"slot_in{i}") for i in range(RING)]
        chunk_in = [sem(f"chunk_in{i}") for i in range(RING)]
        wt_turned = sem("wt_turned")
        bias_spread = sem("bias_spread")
        weights_done = sem("weights_done")
        xh_done = sem("xh_done")
        xl_done = sem("xl_done")
        turned = sem("turned")
        v_turned = sem("v_turned")
        hi_done = sem("hi_done")
        lo_done = sem("lo_done")
        multiplied = sem("multiplied")
        prod_moved = sem("prod_moved")
        prod_turned = sem("prod_turned")
        xg_in = sem("xg_in")
        hg_in = sem("hg_in")
        vchain = sem("vchain")
        stats_done = sem("stats_done")
        gpow = sem("gpow")
        rstd_done = sem("rstd_done")
        xh_rows_used = sem("xh_rows_used")
        x1_done = sem("x1_done")
        x1_out = sem("x1_out")
        x1_turned = sem("x1_turned")
        x1t_moved = sem("x1t_moved")
        heads_done = sem("heads_done")
        heads_moved = sem("heads_moved")
        cols_done = sem("cols_done")
        r_turned = sem("r_turned")
        r_moved = sem("r_moved")

        def wait(eng, s, value):
            if not isinstance(value, int) or value > 0:
                eng.wait_ge(s, value)

        def wait_apart(eng, *waits):
            if all(isinstance(value, int) for _, value in waits):
                for s, value in waits:
                    wait(eng, s, value)
            else:
                held = [(s, eng.to_reg(value)) for s, value in waits]
                eng.wait_ge(const_in, 64)
                for s, value in held:
                    eng.wait_ge(s, value)

        L0 = ExitStack()
        with L0:
            Wn = sb("Wn", [P, F], F32, L0)
            ones = sb("ones", [P, P], F32, L0)
            WTa = sb("WTa", [P, D + 2], F32, L0)
            bias_rows = sb("bias_rows", [P, D + 2], F32, L0)
            bias_wide = sb("bias_wide", [P, D + 2], F32, L0)
            xh = sb("xh", [P, N], F32R, L0)
            xl = sb("xl", [P, N], F32R, L0)
            ah = sb("ah", [P, TB, BANK], F32R, L0)
            al = sb("al", [P, TB, BANK], F32R, L0)
            vt = sb("vt", [P, 2, BANK], F32, L0)
            xg = sb("xg", [P, BANK], F32, L0)
            hg = sb("hg", [P, BANK], F32, L0)
            xhg = sb("xhg", [P, BANK], F32, L0)
            prod = sb("prod", [P, BANK], F32, L0)
            y0 = sb("y0", [P, SUB, F], F32, L0)
            x1 = sb("x1", [P, SUB, F], F32, L0)
            x1T = sb("x1T", [P, BANK], F32, L0)
            sr = sb("sr", [P, SUB, 2], F32, L0)
            st0 = sb("st0", [P, SUB, 6], F32, L0)
            mv0 = sb("mv0", [P, SUB, 2], F32, L0)
            ve0 = sb("ve0", [P, SUB], F32, L0)
            rstd0 = sb("rstd0", [P, SUB], F32, L0)

            PROD, M0, M1, M2 = range(TURN_BANKS, TURN_BANKS + 4)
            PER = SUB // 2
            heads_ps = ps[:, M0:M0 + 2, 0:PER * (D + 2)].rearrange("p b (a c) -> p b a c", a=PER)

            at = {name: k * NB // 64 for name, k in dict(
                move=2, mix=3, turn=5, add=7, stats=9, means=11, norm=16, x1t=20, x1tm=21, heads=24, headm=26,
                rturn=30, rmove=31).items()}

            def buf(k):
                return k % TB

            block = L0.enter_context(nc.Block())

            @block.sync
            def _(sp):
                sp.dma_start(Wn[:, :], W).then_inc(const_in, 16)
                sp.dma_start(bias[:, :], b.rearrange("(d one) -> d one", one=1)).then_inc(const_in, 16)
                sp.dma_start(att[:, 0:1], a_s).then_inc(const_in, 16)
                sp.dma_start(att[:, 1:2], a_r).then_inc(const_in, 16)
                xv = x.rearrange("(b p) f -> p b f", p=P)

                def x_piece(i):
                    to = x_raw[:, i * XPIECE:(i + 1) * XPIECE].rearrange("p (b f) -> p b f", f=F)
                    if i * XBLOCKS < T_BLOCKS:
                        sp.dma_start(to, xv[:, i * XBLOCKS:(i + 1) * XBLOCKS, :]).then_inc(x_in[i], 16)
                    else:
                        for b in range(0, XBLOCKS, BPL):
                            for q in range(P // Q):
                                sp.dma_start(to[q * Q:(q + 1) * Q, b:b + BPL, :],
                                             x_squares[(i * XBLOCKS + b) // BPL, q]).then_inc(x_in[i], 16)

                def loads(g):
                    met = []
                    for kind, c in load_order:
                        first = step_of[kind][c * BPL]
                        if isinstance(g, int) and g == 0:
                            for i in piece_order:
                                if i not in met and first_step[i] <= first + BPL:
                                    x_piece(i)
                                    met.append(i)
                        slot = c % 2 + (2 if kind == "V" else 0)
                        if kind == "T":
                            wait(sp, turned, (g * T_LOADS + c - 1) * BPL)
                            sp.dma_start(load_slot[:, slot], adj_groups[g, :, :, c * JW:(c + 1) * JW])\
                                .then_inc(slot_in[slot], 16)
                        else:
                            wait(sp, v_turned, (g * V_LOADS + c - 1) * BPL)
                            for q in range(P // Q):
                                sp.dma_start(square_slot[q * Q:(q + 1) * Q, slot], adj_squares[g, T_LOADS + c, q])\
                                    .then_inc(slot_in[slot], 16)
                loads(0)
                with sp.Fori(1, GROUPS) as g:
                    loads(g)
                for c in range(RING):
                    if c < 2:
                        sp.wait_ge(turned, (GROUPS * T_LOADS - 1 + c) * BPL)
                    else:
                        sp.wait_ge(v_turned, (GROUPS * V_LOADS - 1 + c - 2) * BPL)
                    sp.dma_start(chunk_slot[:, c], adj_tiles[0, :, c * CW:(c + 1) * CW]).then_inc(chunk_in[c], 16)

            @block.gpsimd
            def _(pool):
                pool.memset(ones[:, :], 1.0).then_inc(ident_done, 1)
                pool.wait_ge(ident_done, 1)
                pool.affine_select(out=ident[:, :], in_=ones[:, :], compare_op=ALU.is_equal, fill=0.0,
                                   base=0, pattern=[[-1, P]], channel_multiplier=1).then_inc(ident_done, 1)
                pool.memset(ones_col[:, :], 1.0)
                pool.memset(power[:, :], -0.5).then_inc(ident_done, 1)

                def rows_in(g):
                    wait(pool, xh_rows_used, g)
                    pool.dma_start(xg[:, :].rearrange("p (a f) -> p a f", a=SUB), x_groups[g]).then_inc(xg_in, 16)
                    pool.dma_start(hg[:, :].rearrange("p (a f) -> p a f", a=SUB), h_groups[g]).then_inc(hg_in, 16)

                def norm_and_store(g):
                    wait_apart(pool, (stats_done, g + 1))
                    pool.tensor_scalar(ve0[:, :], mv0[:, :, 1], EPS, None, ALU.add).then_inc(gpow, 1)
                    pool.wait_ge(gpow, g + 1)
                    pool.tensor_tensor(rstd0[:, :], ve0[:, :], power[:, :], ALU.pow).then_inc(rstd_done, 1)
                    pool.wait_ge(x1_done, g + 1)
                    pool.dma_start(x1_groups[g], x1[:, :, :]).then_inc(x1_out, 16)

                pool.wait_ge(ident_done, 3)
                rows_in(0)
                with pool.Fori(1, GROUPS) as g:
                    rows_in(g)
                    norm_and_store(g - 1)
                norm_and_store(GROUPS - 1)
                pool.wait_ge(x1_out, 16 * GROUPS)

            @block.scalar
            def _(act):
                def x_hi(i):
                    act.wait_ge(x_in[i], 16 if i * XBLOCKS < T_BLOCKS else 16 * (XBLOCKS // BPL) * (P // Q))
                    cols = slice(i * XPIECE, (i + 1) * XPIECE)
                    act.copy(xh[:, cols], x_raw[:, cols]).then_inc(xh_done, 1)

                for i in piece_order[:2]:
                    x_hi(i)
                act.wait_ge(wt_turned, 1)
                act.copy(WTa[:, :], ps[:, M0, 0:D + 2]).then_inc(weights_done, 1)
                act.wait_ge(bias_spread, 1)
                act.copy(bias_wide[:, :], ps[:, M1, 0:D + 2]).then_inc(weights_done, 1)

                def hi(g, k):
                    last = k - TB if k >= TB else max(j for j in range(NB) if buf(j) == buf(k)) - NB
                    wait(act, multiplied, g * NB + last + 1)
                    if kinds[k] == "T":
                        act.wait_ge(turned, g * T_BLOCKS + nth[k] + 1)
                        act.copy(ah[:, buf(k)], ps[:, nth[k] % TURN_BANKS]).then_inc(hi_done, 1)
                    else:
                        act.wait_ge(v_turned, g * V_BLOCKS + nth[k] + 1)
                        act.copy(ah[:, buf(k)], vt[:, nth[k] % 2]).then_inc(hi_done, 1)

                def move(g):
                    act.wait_ge(multiplied, (g + 1) * NB)
                    wait(act, prod_turned, g)
                    act.mul(prod[:, :], ps[:, PROD], 1.0 - MIX).then_inc(prod_moved, 1)

                def move_x1t(g):
                    act.wait_ge(x1_turned, g + 1)
                    act.copy(x1T[:, :], ps[:, M1]).then_inc(x1t_moved, 1)

                def move_r(g):
                    act.wait_ge(r_turned, g + 1)
                    act.copy(r_wide[:, bass.ds(g * BANK, BANK)], ps[:, M2]).then_inc(r_moved, 1)

                def group(g, before):
                    for k in range(NB):
                        hi(g, k)
                        for i in piece_order[2:]:
                            if before is None and k == first_step[i] - XBEFORE:
                                x_hi(i)
                        if before is not None:
                            if k == at["move"]:
                                move(before)
                            if k == at["x1tm"]:
                                move_x1t(before)
                            if k == at["rmove"]:
                                move_r(before)
                group(0, None)
                with act.Fori(1, GROUPS) as g:
                    group(g, g - 1)
                for stage in (move, move_x1t, move_r):
                    stage(GROUPS - 1)

            @block.vector
            def _(dve):
                dve.wait_ge(const_in, 64)
                dve.wait_ge(ident_done, 3)
                dve.tensor_scalar(bias_rows[:, 0:D], ident[:, :], bias[:, 0:1], None, ALU.mult)
                dve.tensor_scalar(bias_rows[:, D:D + 2], att[:, :], bias[:, 0:1], None, ALU.mult)\
                    .then_inc(const_done, 1)

                def x_lo(i):
                    dve.wait_ge(xh_done, piece_order.index(i) + 1)
                    cols = slice(i * XPIECE, (i + 1) * XPIECE)
                    dve.tensor_tensor(xl[:, cols], x_raw[:, cols], xh[:, cols], ALU.subtract).then_inc(xl_done, 1)

                def turn_squares(g, k):
                    c = nth[k] // BPL
                    if nth[k] % BPL == 0:
                        dve.wait_ge(slot_in[2 + c % 2], 16 * (P // Q) * ((V_LOADS // 2) * g + c // 2 + 1))
                    n = nth[k] - 2
                    wait(dve, lo_done, (g - (n < 0)) * NB + step_of["V"][n] + 1)
                    w = (nth[k] % BPL) * Q
                    dve.transpose(vt[:, nth[k] % 2].rearrange("p (m r) -> p m r", r=Q),
                                  square_slot[:, 2 + c % 2, :, w:w + Q]).then_inc(v_turned, 1)

                for i in piece_order[:2]:
                    x_lo(i)

                def lo(g, k):
                    dve.wait_ge(hi_done, g * NB + k + 1)
                    whole = ps[:, nth[k] % TURN_BANKS] if kinds[k] == "T" else vt[:, nth[k] % 2]
                    dve.tensor_tensor(al[:, buf(k)], whole, ah[:, buf(k)], ALU.subtract).then_inc(lo_done, 1)

                def mix(g):
                    dve.wait_ge(xg_in, 16 * (g + 1))
                    dve.wait_ge(hg_in, 16 * (g + 1))
                    dve.scalar_tensor_tensor(out=xhg[:, :], in0=hg[:, :], scalar=MIX, in1=xg[:, :],
                                             op0=ALU.mult, op1=ALU.add).then_inc(xh_rows_used, 1)

                def add(g):
                    dve.wait_ge(xh_rows_used, g + 1)
                    dve.wait_ge(prod_turned, g + 1)
                    dve.tensor_tensor(y0[:, :, :].rearrange("p a f -> p (a f)"), ps[:, M0], xhg[:, :], ALU.add)\
                        .then_inc(vchain, 1)

                def stats(g):
                    dve.wait_ge(vchain, g * (1 + SUB) + 1)
                    for a in range(SUB):
                        dve.bn_stats(st0[:, a, :], y0[:, a, :]).then_inc(vchain, 1)

                def means(g):
                    wait_apart(dve, (vchain, (g + 1) * (1 + SUB)))
                    for a in range(SUB):
                        last = dve.bn_aggr(mv0[:, a, :], st0[:, a, :])
                    last.then_inc(stats_done, 1)

                def norm(g):
                    dve.wait_ge(rstd_done, g + 1)
                    wait(dve, x1_out, 16 * g)
                    for a in range(SUB):
                        last = dve.tensor_scalar(x1[:, a, :], y0[:, a, :], mv0[:, a, 0:1], rstd0[:, a:a + 1],
                                                 ALU.subtract, ALU.mult)
                    last.then_inc(x1_done, 1)

                def move_heads(g):
                    dve.wait_ge(weights_done, 2)
                    dve.wait_ge(heads_done, g + 1)
                    for half in range(2):
                        dve.tensor_tensor(Haug[:, bass.ds(g * SUB + half * PER, PER), 0:D], heads_ps[:, half, :, 0:D],
                                          bias_wide[:, 0:D].unsqueeze(1).broadcast_to([P, PER, D]), ALU.add)
                        last = dve.tensor_tensor(sr[:, half * PER:(half + 1) * PER, :], heads_ps[:, half, :, D:D + 2],
                                                 bias_wide[:, D:D + 2].unsqueeze(1).broadcast_to([P, PER, 2]), ALU.add)
                    last.then_inc(heads_moved, 1)
                    dve.wait_ge(heads_moved, g + 1)
                    dve.tensor_copy(sr_cols[:, bass.ds(g * SUB, SUB), :], sr[:, :, :]).then_inc(cols_done, 1)

                def group(g, before):
                    for k in range(VLEAD):
                        if kinds[k] == "V":
                            turn_squares(g, k)
                    for k in range(NB):
                        if k + VLEAD < NB and kinds[k + VLEAD] == "V":
                            turn_squares(g, k + VLEAD)
                        lo(g, k)
                        for i in piece_order[2:]:
                            if before is None and k == first_step[i] - XBEFORE:
                                x_lo(i)
                        if before is not None:
                            for name, stage in (("mix", mix), ("add", add), ("stats", stats), ("means", means),
                                                ("norm", norm), ("headm", move_heads)):
                                if k == at[name]:
                                    stage(before)
                group(0, None)
                dve.wait_ge(xl_done, XPIECES)
                dve.memset(Haug[:, :, D:HC], 1.0).then_inc(const_done, 1)
                with dve.Fori(1, GROUPS) as g:
                    group(g, g - 1)
                for stage in (mix, add, stats, means, norm, move_heads):
                    stage(GROUPS - 1)
                dve.wait_ge(cols_done, GROUPS)
                dve.tensor_scalar(leak_cols[:, :], sr_cols[:, :, 0], SLOPE, None, ALU.mult)

            @block.tensor
            def _(pe):
                pe.wait_ge(const_in, 64)
                pe.wait_ge(ident_done, 3)
                pe.transpose(ps[:, M0, 0:D], Wn[:, :], ident[:, :])
                pe.matmul(ps[:, M0, D:D + 2], Wn[:, :], att[:, :], start=True, stop=True).then_inc(wt_turned, 1)

                def spread_bias():
                    pe.wait_ge(const_done, 1)
                    pe.matmul(ps[:, M1, 0:D + 2], ones[:, :], bias_rows[:, :], start=True, stop=True)\
                        .then_inc(bias_spread, 1)

                def turn(g, k):
                    c, n = nth[k] // BPL, nth[k] - TURN_BANKS
                    if nth[k] % BPL == 0:
                        pe.wait_ge(slot_in[c % 2], 16 * ((T_LOADS // 2) * g + c // 2 + 1))
                    wait(pe, lo_done, (g - (n < 0)) * NB + step_of["T"][n] + 1)
                    for a in range(SUB):
                        j = (nth[k] % BPL) * P
                        last = pe.transpose(ps[:, nth[k] % TURN_BANKS, a * P:(a + 1) * P],
                                            load_slot[:, c % 2, a, j:j + P], ident[:, :])
                    last.then_inc(turned, 1)

                def multiply(g, k):
                    pe.wait_ge(lo_done, g * NB + k + 1)
                    if isinstance(g, int) and g == 0 and k in first_step:
                        pe.wait_ge(xl_done, piece_order.index(first_step.index(k)) + 1)
                    if k == 0:
                        wait(pe, prod_moved, g)
                    cols = slice(x_block[k] * P, (x_block[k] + 1) * P)
                    pe.matmul(ps[:, PROD], xh[:, cols], ah[:, buf(k)], start=(k == 0), stop=False)
                    pe.matmul(ps[:, PROD], xl[:, cols], ah[:, buf(k)], start=False, stop=False)
                    pe.matmul(ps[:, PROD], xh[:, cols], al[:, buf(k)], start=False, stop=(k == NB - 1))\
                        .then_inc(multiplied, 1)

                def turn_prod(g):
                    pe.wait_ge(prod_moved, g + 1)
                    wait(pe, heads_moved, g)
                    if isinstance(g, int) and g == 0:
                        pe.wait_ge(weights_done, 2)
                    for a in range(SUB):
                        last = pe.transpose(ps[:, M0, a * P:(a + 1) * P], prod[:, a * P:(a + 1) * P], ident[:, :])
                    last.then_inc(prod_turned, 1)

                def turn_x1(g):
                    pe.wait_ge(x1_done, g + 1)
                    for a in range(SUB):
                        last = pe.transpose(ps[:, M1, a * P:(a + 1) * P], x1[:, a, :], ident[:, :])
                    last.then_inc(x1_turned, 1)

                def heads(g):
                    pe.wait_ge(x1t_moved, g + 1)
                    pe.wait_ge(const_done, 2)
                    for a in range(SUB):
                        last = pe.matmul(heads_ps[:, a // PER, a % PER, :], x1T[:, a * P:(a + 1) * P], WTa[:, :],
                                         start=True, stop=True)
                    last.then_inc(heads_done, 1)

                def turn_r(g):
                    pe.wait_ge(heads_moved, g + 1)
                    wait(pe, r_moved, g)
                    for a in range(SUB):
                        last = pe.transpose(ps[:, M2, a * P:(a + 1) * P],
                                            sr[:, a, 1:2].broadcast_to([P, P]), ident[:, :])
                    last.then_inc(r_turned, 1)

                def group(g, before):
                    for k in range(NB):
                        if kinds[k] == "T":
                            turn(g, k)
                        if k >= LAG:
                            multiply(g, k - LAG)
                        elif before is not None:
                            multiply(before, NB - LAG + k)
                        if before is not None:
                            if k == at["turn"]:
                                turn_prod(before)
                            if k == at["x1t"]:
                                turn_x1(before)
                            if k == at["heads"]:
                                heads(before)
                            if k == at["rturn"]:
                                turn_r(before)
                        elif k == 0:
                            spread_bias()
                group(0, None)
                with pe.Fori(1, GROUPS) as g:
                    group(g, g - 1)
                for k in range(NB - LAG, NB):
                    multiply(GROUPS - 1, k)
                for stage in (turn_prod, turn_x1, heads, turn_r):
                    stage(GROUPS - 1)

        leak_done = sem("leak_done")
        leaky_done = sem("leaky_done")
        edges_done = sem("edges_done")
        sign_done = sem("sign_done")
        signed_done = sem("signed_done")
        logits_done = sem("logits_done")
        shift_done = sem("shift_done")
        col_done = sem("col_done")
        bias_done = sem("bias_done")
        plain_exp = sem("plain_exp")
        plain_done = sem("plain_done")
        p_turned = sem("p_turned")
        exp_done = sem("exp_done")
        q_used = sem("q_used")
        x1r_in = [sem(f"x1r_in{i}") for i in range(2)]
        recip_done = sem("recip_done")
        res_done = sem("res_done")
        st_done = sem("st_done")
        mv_done = sem("mv_done")
        eps_done = sem("eps_done")
        rs_done = sem("rs_done")
        normed = sem("normed")
        stored = [sem(f"stored{i}") for i in range(2)]

        L1 = ExitStack()
        with L1:
            t = [sb(f"t{i}", [P, N], F32, L1) for i in range(2)]
            edge = [sb(f"edge{i}", [P, PLAIN * CW], BF16, L1) for i in range(2)]
            pt = sb("pt", [P, 2, QB * P], F32, L1)
            x1r = sb("x1r", [P, 2, F], F32, L1)
            y1 = sb("y1", [P, 2, F], F32, L1)
            o1 = sb("o1", [P, 2, F], F32, L1)
            high = sb("high", [P, 2, CHUNKS], F32, L1)
            shift = sb("shift", [P, 2, P], BF16, L1)
            shift_col = sb("shift_col", [P, 2], BF16, L1)
            shift_bias = sb("shift_bias", [P, 2], F32, L1)
            rden = sb("rden", [P, 2], F32, L1)
            st1 = sb("st1", [P, 2, 6], F32, L1)
            mv1 = sb("mv1", [P, 2, 2], F32, L1)
            ve1 = sb("ve1", [P, 2], F32, L1)
            rstd1 = sb("rstd1", [P, 2], F32, L1)

            quota_ps = ps[:, 0:4, :].rearrange("p (q b) n -> p q (b n)", q=2)
            OUT = 4

            block = L1.enter_context(nc.Block())

            def steps(eng, step):
                for e in range(2):
                    step(e, e)
                with eng.Fori(0, (TILES - 4) // TURNS) as u:
                    for k in range(TURNS):
                        step(TURNS * u + 2 + k, k % 2)
                for e in range(2):
                    step(TILES - 2 + e, e)

            def before(i, e):
                return i // 2 if isinstance(i, int) else (i - e) // 2

            def is_first(i):
                return isinstance(i, int) and i == 0

            def is_last(i):
                return isinstance(i, int) and i == TILES - 1

            def chunk(c):
                return slice(c * CW, (c + 1) * CW)

            @block.sync
            def _(sp):
                def load(i):
                    for c in range(CHUNKS):
                        if c == PLAIN:
                            sp.wait_ge(plain_done, i)
                        else:
                            read = sp.to_reg((i - 1) * CHUNKS + c + 1)
                            if c == SIGNED:
                                sp.wait_ge(sign_done, i)
                            sp.wait_ge(logits_done, read)
                        sp.dma_start(chunk_slot[:, c], adj_tiles[i, :, chunk(c)]).then_inc(chunk_in[c], 16)
                with sp.Fori(1, TILES) as i:
                    load(i)

            @block.gpsimd
            def _(pool):
                def x1_in(i, e):
                    pool.dma_start(x1r[:, e, :], x1_tiles[i]).then_inc(x1r_in[e], 16)

                x1_in(0, 0)
                x1_in(1, 1)

                def finish(i, e):
                    wait_apart(pool, (mv_done, i + 1))
                    pool.tensor_scalar(ve1[:, e:e + 1], mv1[:, e, 1:2], EPS, None, ALU.add).then_inc(eps_done, 1)
                    if not (isinstance(i, int) and i >= TILES - 2):
                        x1_in(i + 2, e)
                    pool.wait_ge(eps_done, i + 1)
                    pool.tensor_tensor(rstd1[:, e:e + 1], ve1[:, e:e + 1], power[:, 0:1], ALU.pow).then_inc(rs_done, 1)
                    wait_apart(pool, (rs_done, i + 1), (stored[e], 16 * before(i, e)))
                    pool.tensor_scalar(o1[:, e, :], y1[:, e, :], mv1[:, e, 0:1], rstd1[:, e:e + 1],
                                       ALU.subtract, ALU.mult).then_inc(normed, 1)
                    wait_apart(pool, (normed, i + 1))
                    pool.dma_start(out_tiles[i], o1[:, e, :]).then_inc(stored[e], 16)
                steps(pool, finish)
                for e in range(2):
                    pool.wait_ge(stored[e], 16 * (TILES // 2))

            @block.scalar
            def _(act):
                def leak(i, e, c):
                    wait_apart(act, (p_turned, (i - 2) * QPT + (c + 1) * QPC))
                    act.activation(t[e][:, chunk(c)], r_wide[:, chunk(c)], ACT.Identity, scale=SLOPE,
                                   bias=leak_cols[:, bass.ds(i, 1)]).then_inc(leak_done, 1)

                def probabilities(i, q):
                    act.wait_ge(p_turned, i * QPT + q + 1)
                    wait(act, q_used, i * QPT + q - 1)
                    if q // QPC == PLAIN:
                        act.copy(pt[:, q % 2], quota_ps[:, q % 2]).then_inc(exp_done, 1)
                    else:
                        act.activation(pt[:, q % 2], quota_ps[:, q % 2], ACT.Exp).then_inc(exp_done, 1)

                def signs(i, e):
                    wait(act, p_turned, (i - 2) * QPT + (SIGNED + 1) * QPC)
                    act.wait_ge(chunk_in[SIGNED], 16 * (i + 1))
                    act.activation(edge[e][:, chunk(SIGNED)], chunk_slot[:, SIGNED], ACT.Sign).then_inc(sign_done, 1)

                def squares(i, e):
                    act.wait_ge(sign_done, i + 1)
                    act.activation(edge[e][:, chunk(SIGNED)], edge[e][:, chunk(SIGNED)], ACT.Square,
                                   scale=ROOT - 1.0, bias=one).then_inc(signed_done, 1)

                def plain(i, e):
                    act.wait_ge(bias_done, i + 1)
                    act.activation(t[e][:, chunk(PLAIN)], t[e][:, chunk(PLAIN)], ACT.Exp,
                                   bias=shift_bias[:, e:e + 1]).then_inc(plain_exp, 1)

                for c in range(CHUNKS):
                    leak(0, 0, c)
                for c in range(AHEAD):
                    leak(1, 1, c)
                signs(0, 0)
                squares(0, 0)

                def step(i, e):
                    for c in range(CHUNKS):
                        for q in range(c * QPC, (c + 1) * QPC):
                            probabilities(i, q)
                            if q == 0:
                                plain(i, e)
                            if q == SIGNS_AT and not is_last(i):
                                signs(i + 1, 1 - e)
                            if q == SQUARES_AT and not is_last(i):
                                squares(i + 1, 1 - e)
                        if c + AHEAD < CHUNKS:
                            if not is_last(i):
                                leak(i + 1, 1 - e, c + AHEAD)
                        elif not (isinstance(i, int) and i >= TILES - 2):
                            leak(i + 2, e, c + AHEAD - CHUNKS)
                steps(act, step)

            @block.vector
            def _(dve):
                def leaky(i, e, c):
                    dve.wait_ge(leak_done, i * CHUNKS + c + 1)
                    dve.scalar_tensor_tensor(out=t[e][:, chunk(c)], in0=r_wide[:, chunk(c)],
                                             scalar=sr_cols[:, bass.ds(i, 1), 0], in1=t[e][:, chunk(c)],
                                             op0=ALU.add, op1=ALU.max).then_inc(leaky_done, 1)

                def edges(i, e, c):
                    dve.wait_ge(chunk_in[c], 16 * (i + 1))
                    wait(dve, p_turned, (i - 2) * QPT + (c + 1) * QPC)
                    dve.tensor_scalar(edge[e][:, chunk(c)], chunk_slot[:, c], 0.0, 1.0 / MASKED_BY,
                                      ALU.is_le, ALU.add).then_inc(edges_done, 1)

                def logits(i, e, c):
                    so_far = [(logits_done, i * CHUNKS + c)] if c > 0 else []
                    wait_apart(dve, (leaky_done, i * CHUNKS + c + 1), (chunk_in[c], 16 * (i + 1)), *so_far)
                    dve.tensor_tensor_reduce(out=t[e][:, chunk(c)], in0=chunk_slot[:, c], in1=t[e][:, chunk(c)],
                                             scale=1.0, scalar=LEAST_SHIFT if c == 0 else high[:, e, c - 1:c],
                                             op0=ALU.mult, op1=ALU.max,
                                             accum_out=high[:, e, c:c + 1]).then_inc(logits_done, 1)

                def shifts(i, e):
                    dve.wait_ge(logits_done, (i + 1) * CHUNKS)
                    highest = high[:, e, CHUNKS - 1:CHUNKS]
                    dve.tensor_scalar(shift[:, e, :], ident[:, :], highest, -MASKED_BY, ALU.mult, ALU.mult)\
                        .then_inc(shift_done, 1)
                    dve.tensor_scalar(shift_col[:, e:e + 1], highest, -MASKED_BY, None, ALU.mult)\
                        .then_inc(col_done, 1)
                    dve.wait_ge(col_done, i + 1)
                    dve.tensor_scalar(shift_bias[:, e:e + 1], shift_col[:, e:e + 1], 1.0 / MASKED_BY, None,
                                      ALU.mult).then_inc(bias_done, 1)

                def mask(i, e):
                    dve.wait_ge(plain_exp, i + 1)
                    dve.scalar_tensor_tensor(out=t[e][:, chunk(PLAIN)], in0=chunk_slot[:, PLAIN], scalar=0.0,
                                             in1=t[e][:, chunk(PLAIN)], op0=ALU.is_gt, op1=ALU.mult)\
                        .then_inc(plain_done, 1)

                def denominators(i, e):
                    dve.wait_ge(q_used, (i + 1) * QPT)
                    dve.reciprocal(rden[:, e:e + 1], ps[:, OUT + e, D:D + 1]).then_inc(recip_done, 1)

                def residual(i, e):
                    dve.wait_ge(recip_done, i + 1)
                    dve.wait_ge(x1r_in[e], 16 * (before(i, e) + 1))
                    wait(dve, normed, i - 1)
                    dve.scalar_tensor_tensor(out=y1[:, e, :], in0=ps[:, OUT + e, 0:D], scalar=rden[:, e:e + 1],
                                             in1=x1r[:, e, :], op0=ALU.mult, op1=ALU.add).then_inc(res_done, 1)

                def statistics(i, e):
                    dve.wait_ge(res_done, i + 1)
                    dve.bn_stats(st1[:, e, :], y1[:, e, :]).then_inc(st_done, 1)

                def moments(i, e):
                    wait_apart(dve, (st_done, i + 1))
                    dve.bn_aggr(mv1[:, e, :], st1[:, e, :]).then_inc(mv_done, 1)

                rows = (denominators, residual, statistics, moments)

                def tile(i, e, finish):
                    for c in range(SIGNED):
                        leaky(i, e, c)
                        if c == 1:
                            finish(residual)
                        edges(i, e, c)
                        if c == 1:
                            finish(statistics)
                        logits(i, e, c)
                        if c == 0:
                            finish(mask)
                            finish(denominators)
                    finish(moments)
                    leaky(i, e, SIGNED)
                    leaky(i, e, PLAIN)
                    logits(i, e, SIGNED)
                    logits(i, e, PLAIN)
                    shifts(i, e)

                tile(0, 0, lambda stage: None)

                def step(i, e):
                    def finish(stage):
                        if stage is mask:
                            mask(i, e)
                        elif not is_first(i):
                            stage(i - 1, 1 - e)

                    if is_last(i):
                        for stage in (mask, *rows):
                            finish(stage)
                    else:
                        tile(i + 1, 1 - e, finish)
                steps(dve, step)
                for stage in rows:
                    stage(TILES - 1, 1)

            @block.tensor
            def _(pe):
                def turn(i, e, q):
                    if q == 0:
                        pe.wait_ge(shift_done, i + 1)
                    if q == SIGNED * QPC:
                        pe.wait_ge(signed_done, i + 1)
                    if q == PLAIN * QPC:
                        pe.wait_ge(plain_done, i + 1)
                    for n in range(QB):
                        col = (q * QB + n) * P
                        to = quota_ps[:, q % 2, n * P:(n + 1) * P]
                        if q // QPC == PLAIN:
                            last = pe.transpose(to, t[e][:, col:col + P], ident[:, :])
                            continue
                        pe.matmul(to, t[e][:, col:col + P], ident[:, :], is_transpose=True, start=True, stop=False)
                        last = pe.matmul(to, edge[e][:, col:col + P], shift[:, e, :], start=False, stop=True)
                    last.then_inc(p_turned, 1)

                def multiply(i, e, q):
                    pe.wait_ge(exp_done, i * QPT + q + 1)
                    if q == 0:
                        wait(pe, res_done, i - 1)
                    for n in range(QB):
                        blk = q * QB + n
                        last = pe.matmul(ps[:, OUT + e, 0:HC], pt[:, q % 2, n * P:(n + 1) * P], Haug[:, blk, :],
                                         start=(blk == 0), stop=(blk == NB - 1))
                    last.then_inc(q_used, 1)

                def step(i, e):
                    for q in range(QPT):
                        turn(i, e, q)
                        if q > 0:
                            multiply(i, e, q - 1)
                        elif not is_first(i):
                            multiply(i - 1, 1 - e, QPT - 1)
                steps(pe, step)
                multiply(TILES - 1, 1, QPT - 1)


_INS = ['x', 'adj', 'L0_gnn_h', 'L1_gnn_W', 'L1_gnn_b', 'L1_gnn_a_s', 'L1_gnn_a_r']


def kernel(**inputs):
    import numpy as _np
    import concourse.bacc as _bacc
    from concourse import mybir as _mybir
    from concourse.bass_utils import run_bass_kernel_spmd as _run

    nc = _bacc.Bacc("TRN2", target_bir_lowering=False, num_devices=1)
    arrays, args = {}, []
    for name in _INS:
        a = _np.ascontiguousarray(inputs[name])
        arrays[f"in_{name}"] = a
        args.append(nc.dram_tensor(f"in_{name}", a.shape, _mybir.dt.from_np(a.dtype), kind="ExternalInput").ap())
    args.append(nc.dram_tensor("out_x", inputs["x"].shape, _mybir.dt.float32, kind="ExternalOutput").ap())
    gnn_kernel(nc, *args)
    r = _run(nc, [arrays], core_ids=[0])
    return r.results[0]["out_x"]
```

```python
from contextlib import ExitStack

import concourse.bass as bass
from concourse import mybir

P = 128
BANK = 512
ALU = mybir.AluOpType
ACT = mybir.ActivationFunctionType
F32 = mybir.dt.float32
F32R = mybir.dt.float32r
BF16 = mybir.dt.bfloat16

MIX = 0.1
SLOPE = 0.2
EPS = 1e-5
LEAST_SHIFT = 1.0
MASKED_BY = 2.0 ** 14


def gnn_kernel(nc, x, adj, h, W, b, a_s, a_r, out):
    N, F = x.shape
    D = W.shape[0]
    assert F == P and D == P and N % 4096 == 0
    NB = N // P

    SUB = BANK // P
    GROUPS = N // BANK
    JW = 512
    LOADS = N // JW
    BPL = JW // P
    RING = 4
    TB = 5
    TURN_BANKS = 4
    LAG = 4
    V_LOADS = 7 * LOADS // 16
    T_LOADS = LOADS - V_LOADS
    V_BLOCKS, T_BLOCKS = V_LOADS * BPL, T_LOADS * BPL
    kinds = ["V" if ((k + 1) * V_BLOCKS + NB // 2) // NB > (k * V_BLOCKS + NB // 2) // NB else "T" for k in range(NB)]
    nth = [kinds[:k].count(kinds[k]) for k in range(NB)]
    step_of = {kind: [k for k in range(NB) if kinds[k] == kind] for kind in "TV"}
    x_block = [nth[k] + (T_BLOCKS if kinds[k] == "V" else 0) for k in range(NB)]
    load_order = sorted(((kind, c) for kind, loads in (("T", T_LOADS), ("V", V_LOADS)) for c in range(loads)),
                        key=lambda load: step_of[load[0]][load[1] * BPL])
    VLEAD = 2
    XBEFORE = 5
    XPIECE = JW
    XBLOCKS = XPIECE // P
    XPIECES = N // XPIECE
    first_step = [min(k for k in range(NB) if x_block[k] // XBLOCKS == i) for i in range(XPIECES)]
    piece_order = sorted(range(XPIECES), key=lambda i: first_step[i])
    Q = 32
    assert GROUPS % 2 == 0

    TILES = NB
    TURNS = 4
    assert (TILES - 4) % TURNS == 0
    CW = N // 4
    CHUNKS = N // CW
    QB = 2 * BANK // P
    QPC = CW // (QB * P)
    QPT = CHUNKS * QPC
    EARLY = 2
    AHEAD = 2
    PLAIN = CHUNKS - 1
    SIGNED = PLAIN - 1
    SIGNS_AT, SQUARES_AT = QPC, 2 * QPC
    ROOT = MASKED_BY ** -0.5
    HC = D + 1

    scratch = nc.dram_tensor("x1_scratch", (N, F), F32, kind="Internal").ap()

    adj_groups = adj.rearrange("(g a p) j -> g p a j", a=SUB, p=P)
    adj_tiles = adj.rearrange("(t p) j -> t p j", p=P)
    adj_squares = adj.rearrange("(g m r) (l q w) -> g l q r m w", m=BANK // Q, r=Q, q=P // Q, w=P)
    x_squares = x.rearrange("(l q s r) f -> l q r s f", q=P // Q, s=JW // P, r=Q)
    x_groups = x.rearrange("(g a p) f -> g p a f", a=SUB, p=P)
    h_groups = h.rearrange("(g a p) f -> g p a f", a=SUB, p=P)
    x1_groups = scratch.rearrange("(g a p) f -> g p a f", a=SUB, p=P)
    x1_tiles = scratch.rearrange("(t p) f -> t p f", p=P)
    out_tiles = out.rearrange("(t p) f -> t p f", p=P)

    with ExitStack() as ctx:
        def sem(name):
            return ctx.enter_context(nc.semaphore(name))

        def sb(name, shape, dt=F32, scope=ctx):
            return scope.enter_context(nc.sbuf_tensor(name, shape, dt))

        ps = ctx.enter_context(nc.psum_tensor("ps", [P, 8, BANK], F32))

        ident = sb("ident", [P, P])
        bias = sb("bias", [P, 1])
        att = sb("att", [P, 2])
        power = sb("power", [P, SUB])
        sr_cols = sb("sr_cols", [P, NB, 2])
        leak_cols = sb("leak_cols", [P, NB])
        r_wide = sb("r_wide", [P, N])
        one = sb("one", [P, 1])
        Haug = sb("Haug", [P, NB, HC])
        a_ring = sb("a_ring", [P, RING * SUB * JW])

        square_slot = a_ring[:, :].rearrange("p (s m w) -> p s m w", s=RING, m=BANK // Q)
        with ExitStack() as place:
            xh = sb("xh", [P, N], F32R, place)
        t = [sb("t0", [P, N])]
        high = sb("high", [P, 2, CHUNKS])
        load_slot = a_ring[:, :].rearrange("p (s a j) -> p s a j", s=RING, a=SUB)
        chunk_slot = a_ring[:, 0:RING * CW].rearrange("p (s j) -> p s j", s=RING)
        x_raw = Haug[:, :, :].rearrange("p b c -> p (b c)")[:, 0:N]

        const_in = sem("const_in")
        x_in = [sem(f"x_in{i}") for i in range(XPIECES)]
        ident_done = sem("ident_done")
        const_done = sem("const_done")
        slot_in = [sem(f"slot_in{i}") for i in range(RING)]
        chunk_in = [sem(f"chunk_in{i}") for i in range(RING)]
        wt_turned = sem("wt_turned")
        bias_spread = sem("bias_spread")
        weights_done = sem("weights_done")
        xh_done = sem("xh_done")
        xl_done = sem("xl_done")
        turned = sem("turned")
        v_turned = sem("v_turned")
        hi_done = sem("hi_done")
        lo_done = sem("lo_done")
        multiplied = sem("multiplied")
        prod_moved = sem("prod_moved")
        prod_turned = sem("prod_turned")
        xg_in = sem("xg_in")
        hg_in = sem("hg_in")
        vchain = sem("vchain")
        stats_done = sem("stats_done")
        gpow = sem("gpow")
        rstd_done = sem("rstd_done")
        xh_rows_used = sem("xh_rows_used")
        x1_done = sem("x1_done")
        x1_out = sem("x1_out")
        x1_turned = sem("x1_turned")
        x1t_moved = sem("x1t_moved")
        heads_done = sem("heads_done")
        heads_moved = sem("heads_moved")
        cols_done = sem("cols_done")
        r_turned = sem("r_turned")
        r_moved = sem("r_moved")
        leak_cols_done = sem("leak_cols_done")
        leak_done = sem("leak_done")
        leaky_done = sem("leaky_done")
        logits_done = sem("logits_done")
        p_turned = sem("p_turned")

        def wait(eng, s, value):
            if not isinstance(value, int) or value > 0:
                eng.wait_ge(s, value)

        def wait_apart(eng, *waits):
            if all(isinstance(value, int) for _, value in waits):
                for s, value in waits:
                    wait(eng, s, value)
            else:
                held = [(s, eng.to_reg(value)) for s, value in waits]
                eng.wait_ge(const_in, 64)
                for s, value in held:
                    eng.wait_ge(s, value)

        def chunk(c):
            return slice(c * CW, (c + 1) * CW)

        def leak(act, i, e, c):
            wait_apart(act, (p_turned, (i - 2) * QPT + (c + 1) * QPC))
            act.activation(t[e][:, chunk(c)], r_wide[:, chunk(c)], ACT.Identity, scale=SLOPE,
                           bias=leak_cols[:, bass.ds(i, 1)]).then_inc(leak_done, 1)

        def leaky(dve, i, e, c):
            dve.wait_ge(leak_done, i * CHUNKS + c + 1)
            dve.scalar_tensor_tensor(out=t[e][:, chunk(c)], in0=r_wide[:, chunk(c)],
                                     scalar=sr_cols[:, bass.ds(i, 1), 0], in1=t[e][:, chunk(c)],
                                     op0=ALU.add, op1=ALU.max).then_inc(leaky_done, 1)

        def logits(dve, i, e, c):
            so_far = [(logits_done, i * CHUNKS + c)] if c > 0 else []
            wait_apart(dve, (leaky_done, i * CHUNKS + c + 1), (chunk_in[c], 16 * (i + 1)), *so_far)
            dve.tensor_tensor_reduce(out=t[e][:, chunk(c)], in0=chunk_slot[:, c], in1=t[e][:, chunk(c)],
                                     scale=1.0, scalar=LEAST_SHIFT if c == 0 else high[:, e, c - 1:c],
                                     op0=ALU.mult, op1=ALU.max,
                                     accum_out=high[:, e, c:c + 1]).then_inc(logits_done, 1)

        L0 = ExitStack()
        with L0:
            Wn = sb("Wn", [P, F], F32, L0)
            ones = sb("ones", [P, P], F32, L0)
            WTa = sb("WTa", [P, D + 2], F32, L0)
            bias_rows = sb("bias_rows", [P, D + 2], F32, L0)
            bias_wide = sb("bias_wide", [P, D + 2], F32, L0)
            xl = sb("xl", [P, N], F32R, L0)
            ah = sb("ah", [P, TB, BANK], F32R, L0)
            al = sb("al", [P, TB, BANK], F32R, L0)
            vt = sb("vt", [P, 2, BANK], F32, L0)
            xg = sb("xg", [P, BANK], F32, L0)
            hg = sb("hg", [P, BANK], F32, L0)
            xhg = sb("xhg", [P, BANK], F32, L0)
            prod = sb("prod", [P, BANK], F32, L0)
            y0 = sb("y0", [P, SUB, F], F32, L0)
            x1 = sb("x1", [P, SUB, F], F32, L0)
            x1T = sb("x1T", [P, BANK], F32, L0)
            sr = sb("sr", [P, SUB, 2], F32, L0)
            st0 = sb("st0", [P, SUB, 6], F32, L0)
            mv0 = sb("mv0", [P, SUB, 2], F32, L0)
            ve0 = sb("ve0", [P, SUB], F32, L0)
            rstd0 = sb("rstd0", [P, SUB], F32, L0)
            away0 = sb("away0", [P, SUB], F32, L0)
            off0 = sb("off0", [P, SUB], F32, L0)

            PROD, M0, M1, M2 = range(TURN_BANKS, TURN_BANKS + 4)
            PER = SUB // 2
            heads_ps = ps[:, M0:M0 + 2, 0:PER * (D + 2)].rearrange("p b (a c) -> p b a c", a=PER)

            at = {name: k * NB // 64 for name, k in dict(
                move=2, mix=3, turn=5, add=7, stats=9, means=11, norm=16, x1t=20, x1tm=21, heads=24, headm=26,
                rturn=30, rmove=31).items()}

            def buf(k):
                return k % TB

            def slot_of(kind, c, odd):
                return (odd * (V_LOADS if kind == "V" else T_LOADS) + c) % 2 + (2 if kind == "V" else 0)

            def slot_loads(kind, c, g, odd):
                per_group = V_LOADS if kind == "V" else T_LOADS
                pairs = g // 2 if isinstance(g, int) else (g - odd) // 2
                return pairs * per_group + (odd * per_group + c) // 2 + 1

            def groups(eng, group):
                group(0, None, 0)
                with eng.Fori(0, GROUPS // 2 - 1) as u:
                    group(2 * u + 1, 2 * u, 1)
                    group(2 * u + 2, 2 * u + 1, 0)
                group(GROUPS - 1, GROUPS - 2, 1)

            WEIGHTS_AT = NB // 4

            block = L0.enter_context(nc.Block())

            @block.sync
            def _(sp):
                xv = x.rearrange("(b p) f -> p b f", p=P)

                def weights():
                    sp.dma_start(Wn[:, :], W).then_inc(const_in, 16)
                    sp.dma_start(bias[:, :], b.rearrange("(d one) -> d one", one=1)).then_inc(const_in, 16)
                    sp.dma_start(att[:, 0:1], a_s).then_inc(const_in, 16)
                    sp.dma_start(att[:, 1:2], a_r).then_inc(const_in, 16)

                def x_piece(i):
                    to = x_raw[:, i * XPIECE:(i + 1) * XPIECE].rearrange("p (b f) -> p b f", f=F)
                    if i * XBLOCKS < T_BLOCKS:
                        sp.dma_start(to, xv[:, i * XBLOCKS:(i + 1) * XBLOCKS, :]).then_inc(x_in[i], 16)
                    else:
                        for q in range(P // Q):
                            sp.dma_start(to[q * Q:(q + 1) * Q], x_squares[i, q]).then_inc(x_in[i], 16)

                def loads(g, before, odd):
                    met = []
                    for kind, c in load_order:
                        first = step_of[kind][c * BPL]
                        if isinstance(g, int) and g == 0:
                            for i in piece_order:
                                if i not in met and first_step[i] <= first:
                                    x_piece(i)
                                    met.append(i)
                            if len(met) == 3:
                                weights()
                                met.append("weights")
                        slot = slot_of(kind, c, odd)
                        if kind == "T":
                            wait(sp, turned, (g * T_LOADS + c - 1) * BPL)
                            sp.dma_start(load_slot[:, slot], adj_groups[g, :, :, c * JW:(c + 1) * JW])\
                                .then_inc(slot_in[slot], 16)
                        else:
                            wait(sp, v_turned, (g * V_LOADS + c - 1) * BPL)
                            for q in range(P // Q):
                                sp.dma_start(square_slot[q * Q:(q + 1) * Q, slot], adj_squares[g, T_LOADS + c, q])\
                                    .then_inc(slot_in[slot], 16)
                groups(sp, loads)
                for c in range(RING):
                    if c < 2:
                        sp.wait_ge(turned, (GROUPS * T_LOADS - 1 + c) * BPL)
                    else:
                        sp.wait_ge(v_turned, (GROUPS * V_LOADS - 1 + c - 2) * BPL)
                    sp.dma_start(chunk_slot[:, c], adj_tiles[0, :, c * CW:(c + 1) * CW]).then_inc(chunk_in[c], 16)

            @block.gpsimd
            def _(pool):
                pool.memset(ones[:, :], 1.0).then_inc(ident_done, 1)
                pool.wait_ge(ident_done, 1)
                pool.affine_select(out=ident[:, :], in_=ones[:, :], compare_op=ALU.is_equal, fill=0.0,
                                   base=0, pattern=[[-1, P]], channel_multiplier=1).then_inc(ident_done, 1)
                pool.memset(one[:, :], 1.0)
                pool.memset(power[:, :], -0.5).then_inc(ident_done, 1)

                def rows_in(g):
                    wait(pool, xh_rows_used, g)
                    pool.dma_start(xg[:, :].rearrange("p (a f) -> p a f", a=SUB), x_groups[g]).then_inc(xg_in, 16)
                    pool.dma_start(hg[:, :].rearrange("p (a f) -> p a f", a=SUB), h_groups[g]).then_inc(hg_in, 16)

                def norm_and_store(g):
                    wait_apart(pool, (stats_done, g + 1))
                    pool.tensor_scalar(ve0[:, :], mv0[:, :, 1], EPS, None, ALU.add).then_inc(gpow, 1)
                    pool.wait_ge(gpow, 3 * g + 1)
                    pool.tensor_tensor(rstd0[:, :], ve0[:, :], power[:, :], ALU.pow).then_inc(gpow, 1)
                    pool.wait_ge(gpow, 3 * g + 2)
                    pool.tensor_tensor(away0[:, :], mv0[:, :, 0], rstd0[:, :], ALU.mult).then_inc(gpow, 1)
                    wait_apart(pool, (gpow, 3 * g + 3))
                    pool.tensor_scalar(off0[:, :], away0[:, :], -1.0, None, ALU.mult).then_inc(rstd_done, 1)
                    pool.wait_ge(x1_done, g + 1)
                    pool.dma_start(x1_groups[g], x1[:, :, :]).then_inc(x1_out, 16)

                pool.wait_ge(ident_done, 3)
                rows_in(0)
                with pool.Fori(1, GROUPS) as g:
                    rows_in(g)
                    norm_and_store(g - 1)
                norm_and_store(GROUPS - 1)
                pool.wait_ge(x1_out, 16 * GROUPS)

            @block.scalar
            def _(act):
                def x_hi(i):
                    act.wait_ge(x_in[i], 16 if i * XBLOCKS < T_BLOCKS else 16 * (P // Q))
                    cols = slice(i * XPIECE, (i + 1) * XPIECE)
                    act.copy(xh[:, cols], x_raw[:, cols]).then_inc(xh_done, 1)

                for i in piece_order[:2]:
                    x_hi(i)

                def weights():
                    act.wait_ge(wt_turned, 1)
                    act.copy(WTa[:, :], ps[:, M0, 0:D + 2]).then_inc(weights_done, 1)
                    act.wait_ge(bias_spread, 1)
                    act.copy(bias_wide[:, :], ps[:, M1, 0:D + 2]).then_inc(weights_done, 1)

                def hi(g, k):
                    last = k - TB if k >= TB else max(j for j in range(NB) if buf(j) == buf(k)) - NB
                    wait(act, multiplied, g * NB + last + 1)
                    if kinds[k] == "T":
                        act.wait_ge(turned, g * T_BLOCKS + nth[k] + 1)
                        act.copy(ah[:, buf(k)], ps[:, nth[k] % TURN_BANKS]).then_inc(hi_done, 1)
                    else:
                        act.wait_ge(v_turned, g * V_BLOCKS + nth[k] + 1)
                        act.copy(ah[:, buf(k)], vt[:, nth[k] % 2]).then_inc(hi_done, 1)

                def move(g):
                    act.wait_ge(multiplied, (g + 1) * NB)
                    wait(act, prod_turned, g)
                    act.mul(prod[:, :], ps[:, PROD], 1.0 - MIX).then_inc(prod_moved, 1)

                def norm(g):
                    act.wait_ge(rstd_done, g + 1)
                    wait(act, x1_out, 16 * g)
                    for a in range(SUB):
                        last = act.activation(x1[:, a, :], y0[:, a, :], ACT.Identity, scale=rstd0[:, a:a + 1],
                                              bias=off0[:, a:a + 1])
                    last.then_inc(x1_done, 1)

                def move_x1t(g):
                    act.wait_ge(x1_turned, g + 1)
                    act.copy(x1T[:, :], ps[:, M1]).then_inc(x1t_moved, 1)

                def move_r(g):
                    act.wait_ge(r_turned, g + 1)
                    act.copy(r_wide[:, bass.ds(g * BANK, BANK)], ps[:, M2]).then_inc(r_moved, 1)

                def group(g, before, odd):
                    for k in range(NB):
                        hi(g, k)
                        for i in piece_order[2:]:
                            if before is None and k == first_step[i] - XBEFORE:
                                x_hi(i)
                        if before is None and k == WEIGHTS_AT + 1:
                            weights()
                        if before is not None:
                            if k == at["move"]:
                                move(before)
                            if k == at["norm"]:
                                norm(before)
                            if k == at["x1tm"]:
                                move_x1t(before)
                            if k == at["rmove"]:
                                move_r(before)
                groups(act, group)
                move(GROUPS - 1)
                act.wait_ge(leak_cols_done, 1)
                act.wait_ge(r_moved, EARLY * CW // BANK)
                for c in range(EARLY):
                    leak(act, 0, 0, c)
                for stage in (norm, move_x1t, move_r):
                    stage(GROUPS - 1)

            @block.vector
            def _(dve):
                def weights():
                    dve.wait_ge(const_in, 64)
                    dve.wait_ge(ident_done, 3)
                    dve.tensor_scalar(bias_rows[:, 0:D], ident[:, :], bias[:, 0:1], None, ALU.mult)
                    dve.tensor_scalar(bias_rows[:, D:D + 2], att[:, :], bias[:, 0:1], None, ALU.mult)\
                        .then_inc(const_done, 1)

                def x_lo(i):
                    dve.wait_ge(xh_done, piece_order.index(i) + 1)
                    cols = slice(i * XPIECE, (i + 1) * XPIECE)
                    dve.tensor_tensor(xl[:, cols], x_raw[:, cols], xh[:, cols], ALU.subtract).then_inc(xl_done, 1)

                def turn_squares(g, k, odd):
                    c = nth[k] // BPL
                    slot = slot_of("V", c, odd)
                    if nth[k] % BPL == 0:
                        dve.wait_ge(slot_in[slot], 16 * (P // Q) * slot_loads("V", c, g, odd))
                    n = nth[k] - 2
                    wait(dve, lo_done, (g - (n < 0)) * NB + step_of["V"][n] + 1)
                    w = (nth[k] % BPL) * Q
                    dve.transpose(vt[:, nth[k] % 2].rearrange("p (m r) -> p m r", r=Q),
                                  square_slot[:, slot, :, w:w + Q]).then_inc(v_turned, 1)

                for i in piece_order[:2]:
                    x_lo(i)

                def lo(g, k):
                    dve.wait_ge(hi_done, g * NB + k + 1)
                    whole = ps[:, nth[k] % TURN_BANKS] if kinds[k] == "T" else vt[:, nth[k] % 2]
                    dve.tensor_tensor(al[:, buf(k)], whole, ah[:, buf(k)], ALU.subtract).then_inc(lo_done, 1)

                def mix(g):
                    dve.wait_ge(xg_in, 16 * (g + 1))
                    dve.wait_ge(hg_in, 16 * (g + 1))
                    dve.scalar_tensor_tensor(out=xhg[:, :], in0=hg[:, :], scalar=MIX, in1=xg[:, :],
                                             op0=ALU.mult, op1=ALU.add).then_inc(xh_rows_used, 1)

                def add(g):
                    dve.wait_ge(xh_rows_used, g + 1)
                    dve.wait_ge(prod_turned, g + 1)
                    dve.tensor_tensor(y0[:, :, :].rearrange("p a f -> p (a f)"), ps[:, M0], xhg[:, :], ALU.add)\
                        .then_inc(vchain, 1)

                def stats(g):
                    dve.wait_ge(vchain, g * (1 + SUB) + 1)
                    for a in range(SUB):
                        dve.bn_stats(st0[:, a, :], y0[:, a, :]).then_inc(vchain, 1)

                def means(g):
                    wait_apart(dve, (vchain, (g + 1) * (1 + SUB)))
                    for a in range(SUB):
                        last = dve.bn_aggr(mv0[:, a, :], st0[:, a, :])
                    last.then_inc(stats_done, 1)

                def move_heads(g):
                    dve.wait_ge(weights_done, 2)
                    dve.wait_ge(heads_done, g + 1)
                    for half in range(2):
                        dve.tensor_tensor(Haug[:, bass.ds(g * SUB + half * PER, PER), 0:D], heads_ps[:, half, :, 0:D],
                                          bias_wide[:, 0:D].unsqueeze(1).broadcast_to([P, PER, D]), ALU.add)
                        last = dve.tensor_tensor(sr[:, half * PER:(half + 1) * PER, :], heads_ps[:, half, :, D:D + 2],
                                                 bias_wide[:, D:D + 2].unsqueeze(1).broadcast_to([P, PER, 2]), ALU.add)
                    last.then_inc(heads_moved, 1)
                    dve.wait_ge(heads_moved, g + 1)
                    dve.tensor_copy(sr_cols[:, bass.ds(g * SUB, SUB), :], sr[:, :, :]).then_inc(cols_done, 1)

                def group(g, before, odd):
                    for k in range(VLEAD):
                        if kinds[k] == "V":
                            turn_squares(g, k, odd)
                    for k in range(NB):
                        if k + VLEAD < NB and kinds[k + VLEAD] == "V":
                            turn_squares(g, k + VLEAD, odd)
                        lo(g, k)
                        for i in piece_order[2:]:
                            if before is None and k == first_step[i] - XBEFORE:
                                x_lo(i)
                        if before is None and k == WEIGHTS_AT - 1:
                            weights()
                        if before is not None:
                            for name, stage in (("mix", mix), ("add", add), ("stats", stats), ("means", means),
                                                ("headm", move_heads)):
                                if k == at[name]:
                                    stage(before)
                    if before is None:
                        dve.wait_ge(xl_done, XPIECES)
                        dve.memset(Haug[:, :, D:HC], 1.0).then_inc(const_done, 1)
                groups(dve, group)
                dve.wait_ge(cols_done, GROUPS - 1)
                dve.tensor_scalar(leak_cols[:, 0:NB - SUB], sr_cols[:, 0:NB - SUB, 0], SLOPE, None, ALU.mult)\
                    .then_inc(leak_cols_done, 1)
                for stage in (mix, add, stats, means):
                    stage(GROUPS - 1)
                leaky(dve, 0, 0, 0)
                logits(dve, 0, 0, 0)
                leaky(dve, 0, 0, 1)
                move_heads(GROUPS - 1)
                logits(dve, 0, 0, 1)
                dve.wait_ge(cols_done, GROUPS)
                dve.tensor_scalar(leak_cols[:, NB - SUB:NB], sr_cols[:, NB - SUB:NB, 0], SLOPE, None, ALU.mult)

            @block.tensor
            def _(pe):
                pe.wait_ge(ident_done, 3)

                def weights():
                    pe.wait_ge(const_in, 64)
                    pe.transpose(ps[:, M0, 0:D], Wn[:, :], ident[:, :])
                    pe.matmul(ps[:, M0, D:D + 2], Wn[:, :], att[:, :], start=True, stop=True).then_inc(wt_turned, 1)
                    pe.wait_ge(const_done, 1)
                    pe.matmul(ps[:, M1, 0:D + 2], ones[:, :], bias_rows[:, :], start=True, stop=True)\
                        .then_inc(bias_spread, 1)

                def turn(g, k, odd):
                    c, n = nth[k] // BPL, nth[k] - TURN_BANKS
                    slot = slot_of("T", c, odd)
                    if nth[k] % BPL == 0:
                        pe.wait_ge(slot_in[slot], 16 * slot_loads("T", c, g, odd))
                    wait(pe, lo_done, (g - (n < 0)) * NB + step_of["T"][n] + 1)
                    for a in range(SUB):
                        j = (nth[k] % BPL) * P
                        last = pe.transpose(ps[:, nth[k] % TURN_BANKS, a * P:(a + 1) * P],
                                            load_slot[:, slot, a, j:j + P], ident[:, :])
                    last.then_inc(turned, 1)

                def multiply(g, k):
                    pe.wait_ge(lo_done, g * NB + k + 1)
                    if isinstance(g, int) and g == 0 and k in first_step:
                        pe.wait_ge(xl_done, piece_order.index(first_step.index(k)) + 1)
                    if k == 0:
                        wait(pe, prod_moved, g)
                    cols = slice(x_block[k] * P, (x_block[k] + 1) * P)
                    pe.matmul(ps[:, PROD], xh[:, cols], ah[:, buf(k)], start=(k == 0), stop=False)
                    pe.matmul(ps[:, PROD], xl[:, cols], ah[:, buf(k)], start=False, stop=False)
                    pe.matmul(ps[:, PROD], xh[:, cols], al[:, buf(k)], start=False, stop=(k == NB - 1))\
                        .then_inc(multiplied, 1)

                def turn_prod(g):
                    pe.wait_ge(prod_moved, g + 1)
                    wait(pe, heads_moved, g)
                    if isinstance(g, int) and g == 0:
                        pe.wait_ge(weights_done, 2)
                    for a in range(SUB):
                        last = pe.transpose(ps[:, M0, a * P:(a + 1) * P], prod[:, a * P:(a + 1) * P], ident[:, :])
                    last.then_inc(prod_turned, 1)

                def turn_x1(g):
                    pe.wait_ge(x1_done, g + 1)
                    for a in range(SUB):
                        last = pe.transpose(ps[:, M1, a * P:(a + 1) * P], x1[:, a, :], ident[:, :])
                    last.then_inc(x1_turned, 1)

                def heads(g):
                    pe.wait_ge(x1t_moved, g + 1)
                    pe.wait_ge(const_done, 2)
                    for a in range(SUB):
                        last = pe.matmul(heads_ps[:, a // PER, a % PER, :], x1T[:, a * P:(a + 1) * P], WTa[:, :],
                                         start=True, stop=True)
                    last.then_inc(heads_done, 1)

                def turn_r(g):
                    pe.wait_ge(heads_moved, g + 1)
                    wait(pe, r_moved, g)
                    for a in range(SUB):
                        last = pe.transpose(ps[:, M2, a * P:(a + 1) * P],
                                            sr[:, a, 1:2].broadcast_to([P, P]), ident[:, :])
                    last.then_inc(r_turned, 1)

                def group(g, before, odd):
                    for k in range(NB):
                        if kinds[k] == "T":
                            turn(g, k, odd)
                        if k >= LAG:
                            multiply(g, k - LAG)
                        elif before is not None:
                            multiply(before, NB - LAG + k)
                        if before is not None:
                            if k == at["turn"]:
                                turn_prod(before)
                            if k == at["x1t"]:
                                turn_x1(before)
                            if k == at["heads"]:
                                heads(before)
                            if k == at["rturn"]:
                                turn_r(before)
                        elif k == WEIGHTS_AT:
                            weights()
                groups(pe, group)
                for k in range(NB - LAG, NB):
                    multiply(GROUPS - 1, k)
                for stage in (turn_prod, turn_x1, heads, turn_r):
                    stage(GROUPS - 1)

        edges_done = sem("edges_done")
        sign_done = sem("sign_done")
        signed_done = sem("signed_done")
        shift_done = sem("shift_done")
        col_done = sem("col_done")
        bias_done = sem("bias_done")
        plain_exp = sem("plain_exp")
        plain_done = sem("plain_done")
        exp_done = sem("exp_done")
        q_used = sem("q_used")
        x1r_in = [sem(f"x1r_in{i}") for i in range(2)]
        recip_done = sem("recip_done")
        res_done = sem("res_done")
        st_done = sem("st_done")
        mv_done = sem("mv_done")
        eps_done = sem("eps_done")
        rs_done = sem("rs_done")
        normed = sem("normed")
        stored = [sem(f"stored{i}") for i in range(2)]

        L1 = ExitStack()
        with L1:
            t.append(sb("t1", [P, N], F32, L1))
            edge = [sb(f"edge{i}", [P, PLAIN * CW], BF16, L1) for i in range(2)]
            pt = sb("pt", [P, 2, QB * P], F32, L1)
            x1r = sb("x1r", [P, 2, F], F32, L1)
            y1 = sb("y1", [P, 2, F], F32, L1)
            o1 = sb("o1", [P, 2, F], F32, L1)
            shift = sb("shift", [P, 2, P], BF16, L1)
            shift_col = sb("shift_col", [P, 2], BF16, L1)
            shift_bias = sb("shift_bias", [P, 2], F32, L1)
            rden = sb("rden", [P, 2], F32, L1)
            st1 = sb("st1", [P, 2, 6], F32, L1)
            mv1 = sb("mv1", [P, 2, 2], F32, L1)
            ve1 = sb("ve1", [P, 2], F32, L1)
            rstd1 = sb("rstd1", [P, 2], F32, L1)

            quota_ps = ps[:, 0:4, :].rearrange("p (q b) n -> p q (b n)", q=2)
            OUT = 4

            block = L1.enter_context(nc.Block())

            def steps(eng, step):
                for e in range(2):
                    step(e, e)
                with eng.Fori(0, (TILES - 4) // TURNS) as u:
                    for k in range(TURNS):
                        step(TURNS * u + 2 + k, k % 2)
                for e in range(2):
                    step(TILES - 2 + e, e)

            def before(i, e):
                return i // 2 if isinstance(i, int) else (i - e) // 2

            def is_first(i):
                return isinstance(i, int) and i == 0

            def is_last(i):
                return isinstance(i, int) and i == TILES - 1

            @block.sync
            def _(sp):
                def load(i):
                    for c in range(CHUNKS):
                        if c == PLAIN:
                            sp.wait_ge(plain_done, i)
                        else:
                            read = sp.to_reg((i - 1) * CHUNKS + c + 1)
                            if c == SIGNED:
                                sp.wait_ge(sign_done, i)
                            if isinstance(i, int) and c < SIGNED:
                                sp.wait_ge(edges_done, c + 1)
                            sp.wait_ge(logits_done, read)
                        sp.dma_start(chunk_slot[:, c], adj_tiles[i, :, chunk(c)]).then_inc(chunk_in[c], 16)
                load(1)
                with sp.Fori(2, TILES) as i:
                    load(i)

            @block.gpsimd
            def _(pool):
                def x1_in(i, e):
                    pool.dma_start(x1r[:, e, :], x1_tiles[i]).then_inc(x1r_in[e], 16)

                x1_in(0, 0)
                x1_in(1, 1)

                def finish(i, e):
                    wait_apart(pool, (mv_done, i + 1))
                    pool.tensor_scalar(ve1[:, e:e + 1], mv1[:, e, 1:2], EPS, None, ALU.add).then_inc(eps_done, 1)
                    if not (isinstance(i, int) and i >= TILES - 2):
                        x1_in(i + 2, e)
                    pool.wait_ge(eps_done, i + 1)
                    pool.tensor_tensor(rstd1[:, e:e + 1], ve1[:, e:e + 1], power[:, 0:1], ALU.pow).then_inc(rs_done, 1)
                    wait_apart(pool, (rs_done, i + 1), (stored[e], 16 * before(i, e)))
                    pool.tensor_scalar(o1[:, e, :], y1[:, e, :], mv1[:, e, 0:1], rstd1[:, e:e + 1],
                                       ALU.subtract, ALU.mult).then_inc(normed, 1)
                    wait_apart(pool, (normed, i + 1))
                    pool.dma_start(out_tiles[i], o1[:, e, :]).then_inc(stored[e], 16)
                steps(pool, finish)
                for e in range(2):
                    pool.wait_ge(stored[e], 16 * (TILES // 2))

            @block.scalar
            def _(act):
                def probabilities(i, q):
                    act.wait_ge(p_turned, i * QPT + q + 1)
                    wait(act, q_used, i * QPT + q - 1)
                    if q // QPC == PLAIN:
                        act.copy(pt[:, q % 2], quota_ps[:, q % 2]).then_inc(exp_done, 1)
                    else:
                        act.activation(pt[:, q % 2], quota_ps[:, q % 2], ACT.Exp).then_inc(exp_done, 1)

                def signs(i, e):
                    wait(act, p_turned, (i - 2) * QPT + (SIGNED + 1) * QPC)
                    act.wait_ge(chunk_in[SIGNED], 16 * (i + 1))
                    act.activation(edge[e][:, chunk(SIGNED)], chunk_slot[:, SIGNED], ACT.Sign).then_inc(sign_done, 1)

                def squares(i, e):
                    act.wait_ge(sign_done, i + 1)
                    act.activation(edge[e][:, chunk(SIGNED)], edge[e][:, chunk(SIGNED)], ACT.Square,
                                   scale=ROOT - 1.0, bias=one[:, 0:1]).then_inc(signed_done, 1)

                def plain(i, e):
                    act.wait_ge(bias_done, i + 1)
                    act.activation(t[e][:, chunk(PLAIN)], t[e][:, chunk(PLAIN)], ACT.Exp,
                                   bias=shift_bias[:, e:e + 1]).then_inc(plain_exp, 1)

                for c in range(EARLY, CHUNKS):
                    leak(act, 0, 0, c)
                for c in range(AHEAD):
                    leak(act, 1, 1, c)
                signs(0, 0)
                squares(0, 0)

                def step(i, e):
                    for c in range(CHUNKS):
                        for q in range(c * QPC, (c + 1) * QPC):
                            probabilities(i, q)
                            if q == 0:
                                plain(i, e)
                            if q == SIGNS_AT and not is_last(i):
                                signs(i + 1, 1 - e)
                            if q == SQUARES_AT and not is_last(i):
                                squares(i + 1, 1 - e)
                        if c + AHEAD < CHUNKS:
                            if not is_last(i):
                                leak(act, i + 1, 1 - e, c + AHEAD)
                        elif not (isinstance(i, int) and i >= TILES - 2):
                            leak(act, i + 2, e, c + AHEAD - CHUNKS)
                steps(act, step)

            @block.vector
            def _(dve):
                def edges(i, e, c):
                    dve.wait_ge(chunk_in[c], 16 * (i + 1))
                    wait(dve, p_turned, (i - 2) * QPT + (c + 1) * QPC)
                    dve.tensor_scalar(edge[e][:, chunk(c)], chunk_slot[:, c], 0.0, 1.0 / MASKED_BY,
                                      ALU.is_le, ALU.add).then_inc(edges_done, 1)

                def shifts(i, e):
                    dve.wait_ge(logits_done, (i + 1) * CHUNKS)
                    highest = high[:, e, CHUNKS - 1:CHUNKS]
                    dve.tensor_scalar(shift[:, e, :], ident[:, :], highest, -MASKED_BY, ALU.mult, ALU.mult)\
                        .then_inc(shift_done, 1)
                    dve.tensor_scalar(shift_col[:, e:e + 1], highest, -MASKED_BY, None, ALU.mult)\
                        .then_inc(col_done, 1)
                    dve.wait_ge(col_done, i + 1)
                    dve.tensor_scalar(shift_bias[:, e:e + 1], shift_col[:, e:e + 1], 1.0 / MASKED_BY, None,
                                      ALU.mult).then_inc(bias_done, 1)

                def mask(i, e):
                    dve.wait_ge(plain_exp, i + 1)
                    dve.scalar_tensor_tensor(out=t[e][:, chunk(PLAIN)], in0=chunk_slot[:, PLAIN], scalar=0.0,
                                             in1=t[e][:, chunk(PLAIN)], op0=ALU.is_gt, op1=ALU.mult)\
                        .then_inc(plain_done, 1)

                def denominators(i, e):
                    dve.wait_ge(q_used, (i + 1) * QPT)
                    dve.reciprocal(rden[:, e:e + 1], ps[:, OUT + e, D:D + 1]).then_inc(recip_done, 1)

                def residual(i, e):
                    dve.wait_ge(recip_done, i + 1)
                    dve.wait_ge(x1r_in[e], 16 * (before(i, e) + 1))
                    wait(dve, normed, i - 1)
                    dve.scalar_tensor_tensor(out=y1[:, e, :], in0=ps[:, OUT + e, 0:D], scalar=rden[:, e:e + 1],
                                             in1=x1r[:, e, :], op0=ALU.mult, op1=ALU.add).then_inc(res_done, 1)

                def statistics(i, e):
                    dve.wait_ge(res_done, i + 1)
                    dve.bn_stats(st1[:, e, :], y1[:, e, :]).then_inc(st_done, 1)

                def moments(i, e):
                    wait_apart(dve, (st_done, i + 1))
                    dve.bn_aggr(mv1[:, e, :], st1[:, e, :]).then_inc(mv_done, 1)

                rows = (denominators, residual, statistics, moments)

                def tile(i, e, finish):
                    for c in range(SIGNED):
                        leaky(dve, i, e, c)
                        if c == 1:
                            finish(residual)
                        edges(i, e, c)
                        if c == 1:
                            finish(statistics)
                        logits(dve, i, e, c)
                        if c == 0:
                            finish(mask)
                            finish(denominators)
                    finish(moments)
                    leaky(dve, i, e, SIGNED)
                    leaky(dve, i, e, PLAIN)
                    logits(dve, i, e, SIGNED)
                    logits(dve, i, e, PLAIN)
                    shifts(i, e)

                for c in range(SIGNED):
                    edges(0, 0, c)
                for c in range(EARLY, CHUNKS):
                    leaky(dve, 0, 0, c)
                for c in range(EARLY, CHUNKS):
                    logits(dve, 0, 0, c)
                shifts(0, 0)

                def step(i, e):
                    def finish(stage):
                        if stage is mask:
                            mask(i, e)
                        elif not is_first(i):
                            stage(i - 1, 1 - e)

                    if is_last(i):
                        for stage in (mask, *rows):
                            finish(stage)
                    else:
                        tile(i + 1, 1 - e, finish)
                steps(dve, step)
                for stage in rows:
                    stage(TILES - 1, 1)

            @block.tensor
            def _(pe):
                def turn(i, e, q):
                    if q == 0:
                        pe.wait_ge(shift_done, i + 1)
                    if q == SIGNED * QPC:
                        pe.wait_ge(signed_done, i + 1)
                    if q == PLAIN * QPC:
                        pe.wait_ge(plain_done, i + 1)
                    for n in range(QB):
                        col = (q * QB + n) * P
                        to = quota_ps[:, q % 2, n * P:(n + 1) * P]
                        if q // QPC == PLAIN:
                            last = pe.transpose(to, t[e][:, col:col + P], ident[:, :])
                            continue
                        pe.matmul(to, t[e][:, col:col + P], ident[:, :], is_transpose=True, start=True, stop=False)
                        last = pe.matmul(to, edge[e][:, col:col + P], shift[:, e, :], start=False, stop=True)
                    last.then_inc(p_turned, 1)

                def multiply(i, e, q):
                    pe.wait_ge(exp_done, i * QPT + q + 1)
                    if q == 0:
                        wait(pe, res_done, i - 1)
                    for n in range(QB):
                        blk = q * QB + n
                        last = pe.matmul(ps[:, OUT + e, 0:HC], pt[:, q % 2, n * P:(n + 1) * P], Haug[:, blk, :],
                                         start=(blk == 0), stop=(blk == NB - 1))
                    last.then_inc(q_used, 1)

                def step(i, e):
                    for q in range(QPT):
                        turn(i, e, q)
                        if q > 0:
                            multiply(i, e, q - 1)
                        elif not is_first(i):
                            multiply(i - 1, 1 - e, QPT - 1)
                steps(pe, step)
                multiply(TILES - 1, 1, QPT - 1)


_INS = ['x', 'adj', 'L0_gnn_h', 'L1_gnn_W', 'L1_gnn_b', 'L1_gnn_a_s', 'L1_gnn_a_r']


def kernel(**inputs):
    import numpy as _np
    import concourse.bacc as _bacc
    from concourse import mybir as _mybir
    from concourse.bass_utils import run_bass_kernel_spmd as _run

    nc = _bacc.Bacc("TRN2", target_bir_lowering=False, num_devices=1)
    arrays, args = {}, []
    for name in _INS:
        a = _np.ascontiguousarray(inputs[name])
        arrays[f"in_{name}"] = a
        args.append(nc.dram_tensor(f"in_{name}", a.shape, _mybir.dt.from_np(a.dtype), kind="ExternalInput").ap())
    args.append(nc.dram_tensor("out_x", inputs["x"].shape, _mybir.dt.float32, kind="ExternalOutput").ap())
    gnn_kernel(nc, *args)
    r = _run(nc, [arrays], core_ids=[0])
    return r.results[0]["out_x"]
```
